# Optimizing a Trainium2 kernel written in Bass

```python
import numpy as np
import jax
import jax.numpy as jnp

def _softmax(x, axis=-1):
    return jax.nn.softmax(x, axis=axis)

def _gelu(x):
    return jax.nn.gelu(x, approximate=True)

def _silu(x):
    return jax.nn.silu(x)

def _sigmoid(x):
    return jax.nn.sigmoid(x)

def _layernorm(x, axis=-1, eps=1e-05):
    m = jnp.mean(x, axis=axis, keepdims=True)
    v = jnp.var(x, axis=axis, keepdims=True)
    return (x - m) / jnp.sqrt(v + eps)

def _scatter_add(tgt, idx, src, axis=0):
    return tgt.at[idx].add(src)

def _segment_sum(src, seg, n):
    return jax.ops.segment_sum(src, seg, n)
kernel_name = 'mk_gnn_ffn_d1_gnn_r8_8d9202'

def setup_inputs(seed: int=0):
    np.random.seed(seed)
    _w = jnp.asarray

    def _rec_inputs():
        import jax
        import jax.numpy as jnp
        _gk = jax.random.key(seed)
        x = -0.0002117 + 1 * jax.random.normal(jax.random.fold_in(_gk, 1), (6250, 256), jnp.float32)
        _s = jax.random.randint(jax.random.fold_in(_gk, 2), (100000,), 0, 6250, jnp.int32)
        _d = jax.random.randint(jax.random.fold_in(_gk, 3), (100000,), 0, 6250, jnp.int32)
        _loop = jnp.arange(6250, dtype=jnp.int32)
        src = jnp.concatenate([_s, _d, _loop])
        dst = jnp.concatenate([_d, _s, _loop])
        _o = jnp.argsort(dst, stable=True)
        src = src[_o]
        dst = dst[_o]
        return (x, src, dst)
    x, src, dst = _rec_inputs()

    def _L0_gnn_setup():
        import jax, jax.numpy as jnp
        import numpy as np
        key = jax.random.key(seed)
        k0, k1, k2 = jax.random.split(key, 3)
        N, E, C_IN, C_HID = (12500, 200000, 256, 256)
        x = jax.random.normal(k0, (N, C_IN), dtype=jnp.float32)
        edge_index = jax.random.randint(k1, (2, E), 0, N, dtype=jnp.int64)
        W = jax.random.normal(k2, (C_IN, C_HID), dtype=jnp.float32) / np.sqrt(C_IN).astype(np.float32)
        b = jnp.zeros((C_HID,), dtype=jnp.float32)
        prelu_a = jnp.full((C_HID,), 0.25, dtype=jnp.float32)
        return {'x': x, 'edge_index': edge_index, 'k_centers': 7, 'W': W, 'b': b, 'prelu_a': prelu_a}
    _L0_gnn_all = _L0_gnn_setup()
    _L0_gnn_in = {k: v for k, v in _L0_gnn_all.items() if k in ('W', 'b', 'prelu_a')}
    del _L0_gnn_all

    def _L0_ffn_setup():
        import math
        import jax, jax.numpy as jnp
        import numpy as np
        CAPACITY_FACTOR = 1.25
        TOP_K = 2
        LN_EPS = 1e-05

        def _layer_norm(x, gamma, beta):
            mu = jnp.mean(x, axis=-1, keepdims=True)
            var = jnp.var(x, axis=-1, keepdims=True)
            return (x - mu) * jax.lax.rsqrt(var + LN_EPS) * gamma + beta
        key = jax.random.key(seed)
        ks = jax.random.split(key, 4)
        B, S, D, F, E = (8, 512, 256, 512, 8)
        x = jax.random.normal(ks[0], (B, S, D), dtype=jnp.float32)
        Wr = jax.random.normal(ks[1], (D, E), dtype=jnp.float32) / np.sqrt(D)
        br = jnp.zeros((E,), jnp.float32)
        W1 = jax.random.normal(ks[2], (E, D, F), dtype=jnp.float32) / np.sqrt(D)
        b1 = jnp.zeros((E, F), jnp.float32)
        W2 = jax.random.normal(ks[3], (E, F, D), dtype=jnp.float32) / np.sqrt(F)
        b2 = jnp.zeros((E, D), jnp.float32)
        gamma = jnp.ones((D,), jnp.float32)
        beta = jnp.zeros((D,), jnp.float32)
        return {'x': x, 'Wr': Wr, 'br': br, 'W1': W1, 'b1': b1, 'W2': W2, 'b2': b2, 'gamma': gamma, 'beta': beta}
    _L0_ffn_all = _L0_ffn_setup()
    _L0_ffn_in = {k: v for k, v in _L0_ffn_all.items() if k in ('Wr', 'br', 'W1', 'b1', 'W2', 'b2', 'gamma', 'beta')}
    del _L0_ffn_all
    return {'x': x, 'src': src, 'dst': dst, 'L0_gnn_W': _L0_gnn_in['W'], 'L0_gnn_b': _L0_gnn_in['b'], 'L0_gnn_prelu_a': _L0_gnn_in['prelu_a'], 'L0_ffn_Wr': _L0_ffn_in['Wr'], 'L0_ffn_br': _L0_ffn_in['br'], 'L0_ffn_W1': _L0_ffn_in['W1'], 'L0_ffn_b1': _L0_ffn_in['b1'], 'L0_ffn_W2': _L0_ffn_in['W2'], 'L0_ffn_b2': _L0_ffn_in['b2'], 'L0_ffn_gamma': _L0_ffn_in['gamma'], 'L0_ffn_beta': _L0_ffn_in['beta']}

def reference(x, src, dst, L0_gnn_W, L0_gnn_b, L0_gnn_prelu_a, L0_ffn_Wr, L0_ffn_br, L0_ffn_W1, L0_ffn_b1, L0_ffn_W2, L0_ffn_b2, L0_ffn_gamma, L0_ffn_beta):
    import jax
    import jax.numpy as jnp

    def _L0_gnn_ref(x, edge_index, k_centers, W, b, prelu_a):
        import jax, jax.numpy as jnp
        import numpy as np
        N = x.shape[0]
        loop = jnp.arange(N, dtype=edge_index.dtype)
        src = jnp.concatenate([edge_index[0], loop])
        dst = jnp.concatenate([edge_index[1], loop])
        deg = jax.ops.segment_sum(jnp.ones_like(dst, dtype=x.dtype), dst, num_segments=N)
        dinv = jnp.where(deg > 0, jax.lax.rsqrt(deg), jnp.zeros_like(deg))
        norm = dinv[src] * dinv[dst]
        h = x @ W
        out = jax.ops.segment_sum(h[src] * norm[:, None], dst, num_segments=N) + b
        return jnp.where(out > 0, out, prelu_a * out)

    def _L0_ffn_ref(x, Wr, br, W1, b1, W2, b2, gamma, beta):
        import math
        import jax, jax.numpy as jnp
        import numpy as np
        CAPACITY_FACTOR = 1.25
        TOP_K = 2
        LN_EPS = 1e-05

        def _layer_norm(x, gamma, beta):
            mu = jnp.mean(x, axis=-1, keepdims=True)
            var = jnp.var(x, axis=-1, keepdims=True)
            return (x - mu) * jax.lax.rsqrt(var + LN_EPS) * gamma + beta
        B, S, D = x.shape
        E = Wr.shape[1]
        N = B * S
        K = TOP_K
        logits = jnp.mean(x, axis=1) @ Wr + br
        routing_weights = jax.nn.softmax(logits, axis=-1)
        capacity = float(math.ceil(N * CAPACITY_FACTOR / E))
        expected_loads = routing_weights.sum(axis=0) * (N / B)
        scale = jnp.where(expected_loads > capacity, capacity / expected_loads, 1.0)
        routing_weights = jax.nn.softmax(routing_weights * scale, axis=-1)
        rw_tok = jnp.broadcast_to(routing_weights[:, None, :], (B, S, E)).reshape(N, E)
        top_w, top_i = jax.lax.top_k(rw_tok, K)
        top_w = jax.nn.softmax(top_w, axis=-1)
        xf = x.reshape(N, D)
        h = jax.nn.gelu(jnp.einsum('nd,edf->enf', xf, W1) + b1[:, None, :], approximate=False)
        y = jnp.einsum('enf,efd->end', h, W2) + b2[:, None, :]
        w_dense = jnp.zeros((N, E), x.dtype).at[jnp.arange(N)[:, None], top_i].add(top_w)
        out = jnp.einsum('ne,end->nd', w_dense, y).reshape(B, S, D)
        out = _layer_norm(out + x, gamma, beta)
        return out
    edge_index = jnp.stack([src, dst])
    x = x + _L0_gnn_ref(_layernorm(x, axis=-1), edge_index, 7, L0_gnn_W, L0_gnn_b, L0_gnn_prelu_a)
    x = x + _L0_ffn_ref(_layernorm(x, axis=-1)[None], L0_ffn_Wr, L0_ffn_br, L0_ffn_W1, L0_ffn_b1, L0_ffn_W2, L0_ffn_b2, L0_ffn_gamma, L0_ffn_beta)[0]
    return x

_drawn_inputs = setup_inputs


def setup_inputs(seed=0):
    import zlib

    import numpy as np

    out = dict(_drawn_inputs(seed))
    spreads = {'L0_gnn_b': (0.0, 0.1),
     'L0_gnn_prelu_a': (0.25, 0.6),
     'L0_ffn_br': (0.0, 0.1),
     'L0_ffn_b1': (0.0, 0.373),
     'L0_ffn_b2': (0.0, 0.1),
     'L0_ffn_gamma': (1.0, 0.2),
     'L0_ffn_beta': (0.0, 0.1)}
    factors = {'L0_ffn_Wr': 8.0}
    for name, (base, spread) in spreads.items():
        noise = np.random.default_rng([zlib.crc32(name.encode()), seed]).standard_normal(out[name].shape)
        drawn = base * np.exp(spread * noise) if base else spread * noise
        out[name] = jnp.asarray(drawn.astype(out[name].dtype))
    for name, factor in factors.items():
        out[name] = (out[name] * factor).astype(out[name].dtype)
    return out
```

```python
from contextlib import ExitStack

import concourse.bass as bass
from concourse import mybir

ALU = mybir.AluOpType
ACT = mybir.ActivationFunctionType
AXX = mybir.AxisListType.X
F32 = mybir.dt.float32
BF16 = mybir.dt.bfloat16
I32 = mybir.dt.int32
U32 = mybir.dt.uint32
ds = bass.ds

P = 128
LN_EPS = 1e-5
CAPACITY_FACTOR = 1.25
TOP_K = 2

U = 9
PARTS = ((0, 3), (3, 6), (6, 9))
RANGE = 52
HB = 13


def edge_columns(E):
    return -(-(-(-E // P)) // RANGE) * RANGE


def padded_edges(E):
    return P * edge_columns(E) + P * U


def gnn_ffn_kernel(nc, a, out, E):
    x, src, dst = a["x"], a["src"], a["dst"]
    N, D = x.shape
    NX, _, F = a["W1"].shape
    T = -(-N // P)
    REST = N - (T - 1) * P
    KD, KF = D // P, F // P
    COLS = edge_columns(E)
    EDGES = P * COLS
    NRANGE = COLS // RANGE
    STEPS = COLS // HB
    BATCH = P * U
    MAXB = -(-EDGES // BATCH) + 1
    BIG = float(EDGES)
    CAP = float(-(-N * CAPACITY_FACTOR // NX))
    GT = 3
    NG = (T - 1) // GT
    assert T == NG * GT + 1 and NG % 2 == 0 and T % 7 == 0 and STEPS % 2 == 0

    h_table = nc.dram_tensor("h_table", (T * P, D), F32, kind="Internal").ap()

    with ExitStack() as ctx:
        def sb(name, shape, dt=F32):
            return ctx.enter_context(nc.sbuf_tensor(name, shape, dt))

        def sem(name):
            return ctx.enter_context(nc.semaphore(name))

        xs = sb("xs", [P, T, D])
        hs = sb("hs", [P, T, D])
        zT = sb("zT", [P, KD, T * P])
        ident = sb("ident", [P, P])
        iota = sb("iota", [P, P])
        ones = sb("ones", [P, P])
        zero = sb("zero", [P, P])
        valid = sb("valid", [P, T])
        dinv = sb("dinv", [P, T])
        eps = sb("eps", [P, 1])
        neg_half = sb("neg_half", [P, 1])
        bias_bc = sb("bias_bc", [P, D])
        slope_bc = sb("slope_bc", [P, D])
        gamma_bc = sb("gamma_bc", [P, D])
        beta_bc = sb("beta_bc", [P, D])
        W = sb("W", [P, KD, D])
        Wr = sb("Wr", [P, KD, NX])
        br = sb("br", [1, NX])
        table = sb("table", [1, 3, T], I32)
        block_node = sb("block_node", [P, T])

        arena = sb("arena", [P, TOP_K * (KD * F + KF * D)])

        def carve(flat):
            used = [0]

            def take(n, dt=F32):
                at, used[0] = used[0], used[0] + n
                assert used[0] <= flat.shape[1]
                return flat[:, at:at + n] if dt == F32 else flat[:, at:at + n].bitcast(dt)
            return take

        room = carve(arena[:, :])
        rows = room(U * D).rearrange("p (u d) -> p u d", u=U)
        onehot = room(U * P).rearrange("p (u n) -> p u n", u=U)
        room = carve(arena[:, :])
        xn, xnT = (room(2 * D).rearrange("p (k d) -> p k d", k=2) for _ in range(2))
        room = carve(arena[:, :])
        W1e = room(TOP_K * KD * F).rearrange("p (e k f) -> p e k f", e=TOP_K, k=KD)
        W2e = room(TOP_K * KF * D).rearrange("p (e k d) -> p e k d", e=TOP_K, k=KF)
        src_ix = [sb(f"src_ix{h}", [P, hi - lo], I32) for h, (lo, hi) in enumerate(PARTS)]
        dst_ix = sb("dst_ix", [P, U], I32)
        dst_loc = sb("dst_loc", [P, U])

        mv = sb("mv", [P, T, 2])
        sd = sb("sd", [P, T])
        rstd = sb("rstd", [P, T])
        stats = sb("stats", [P, 6])
        agg = sb("agg", [P, D])
        neg = sb("neg", [P, D])
        zst = sb("zst", [P, D])

        hT = sb("hT", [P, 2, TOP_K, KF, GT * P])
        b1e = sb("b1e", [P, TOP_K, KF])
        b2e = sb("b2e", [P, TOP_K, D])
        b2w = sb("b2w", [P, D])
        res = sb("res", [P, 2, D])
        route = sb("route", [1, 12, NX])
        route_ix = sb("route_ix", [1, 8], U32)
        zmean = sb("zmean", [P, KD])
        wts = sb("wts", [P, TOP_K])

        gmin = sb("gmin", [P, NRANGE])
        gmax = sb("gmax", [P, NRANGE])
        gpos = sb("gpos", [P, NRANGE])
        lim = sb("lim", [P, 2, T])
        span = sb("span", [T, 4])
        before = sb("before", [T, T])

        z_room = carve(zT[:, :, :].rearrange("p k n -> p (k n)"))
        dst_all, low_i, high_i = (z_room(COLS, I32) for _ in range(3))
        low, high = z_room(COLS), z_room(COLS)
        h_room = carve(hT[:, :, :, :, :].rearrange("p a b c n -> p (a b c n)"))
        hot_low = h_room(HB * P, BF16).rearrange("p (k c n) -> p k c n", k=2, c=HB)
        hot_high = h_room(HB * T, BF16).rearrange("p (k c n) -> p k c n", k=2, c=HB)
        hit, cand = (h_room(T * NRANGE).rearrange("p (t g) -> p t g", t=T) for _ in range(2))
        batch_starts, over = h_room(MAXB)[0:T, :], h_room(MAXB)[0:T, :]

        banks = [ctx.enter_context(nc.psum_tensor(f"bank{i}", [P, 512], F32)) for i in range(8)]
        acc, zsum, turn, rt_ps, deg = banks[0], banks[1], banks[2], banks[3], banks[4]
        turn_ps = [banks[2], banks[3]]
        h_ps = [banks[0], banks[1]]
        lim_ps = [banks[5], banks[6]]
        table_ps = [banks[7][0:1, 128 * k:128 * k + T] for k in range(3)]
        h1_ps = banks[2:6]
        y_ps = banks[6:8]

        consts = sem("consts")
        held = sem("held")
        pad_zero = sem("pad_zero")
        x_parts = [(0, 12), (12, 24), (24, 36), (36, T - 1)]
        x_in = [sem(f"x_in{i}") for i in range(len(x_parts) + 1)]
        edges_in = sem("edges_in")
        weights_in = sem("weights_in")
        dve_pro = sem("dve_pro")
        sd_made = sem("sd_made")
        xn_ready = sem("xn_ready")
        xn_turned = sem("xn_turned")
        xnT_ready = sem("xnT_ready")
        h_made = sem("h_made")
        h_kept = sem("h_kept")
        hot_ready = sem("hot_ready")
        hot_used = sem("hot_used")
        deg_ready = sem("deg_ready")
        h_scaled = sem("h_scaled")
        h_stored = sem("h_stored")
        lim_turned = sem("lim_turned")
        table_made = sem("table_made")
        table_ready = sem("table_ready")
        src_in = [sem(f"src_in{h}") for h in range(len(PARTS))]
        dst_in = sem("dst_in")
        dst_free = sem("dst_free")
        rows_in = [sem(f"rows_in{u}") for u in range(U)]
        loc_ready = sem("loc_ready")
        onehot_ready = sem("onehot_ready")
        slot_free = sem("slot_free")
        epi = sem("epi")
        sd2_made = sem("sd2_made")
        z_turned = sem("z_turned")
        z_kept = sem("z_kept")
        zsum_ready = sem("zsum_ready")
        rt = sem("rt")
        rt_pe = sem("rt_pe")
        rt_act = sem("rt_act")
        experts_in = sem("experts_in")
        h1_made = sem("h1_made")
        h1_kept = sem("h1_kept")
        y_made = sem("y_made")
        fin = sem("fin")
        pow_ready = sem("pow_ready")
        res_stored = [sem(f"res_stored{k}") for k in range(2)]

        CONSTS = 14
        N_WEIGHTS = 16 * 7
        EPI = 8
        FIN = 9
        ROUTE_IX, ROUTE_W, ROUTE_END = 18, 23, 27
        Y_SLOTS = 2 * GT

        STATS = 2 * T
        LIM = STATS + 1 + 6 + 7
        SPAN = LIM + 6
        DINV = SPAN + 4

        block = ctx.enter_context(nc.Block())

        def block_edges(eng, d):
            return (eng.value_load(table[0:1, 0, ds(d, 1)], min_val=0, max_val=EDGES),
                    eng.value_load(table[0:1, 1, ds(d, 1)], min_val=1, max_val=MAXB),
                    eng.value_load(table[0:1, 2, ds(d, 1)], min_val=0, max_val=MAXB * T))

        def hold(eng, semaphore, value):
            eng.wait_ge(semaphore, value)
            eng.sem_inc(held, 1)

        def tile(buf, t):
            return buf[:, ds(t, 1), :].rearrange("p o d -> p (o d)")

        @block.sync
        def _(sp):
            sp.dma_start(dst_all, dst[0:EDGES].rearrange("(p c) -> p c", p=P)).then_inc(edges_in, 16)
            for i, (lo, hi) in enumerate(x_parts):
                sp.dma_start(xs[:, lo:hi, :], x[lo * P:hi * P, :].rearrange("(t p) d -> p t d", p=P)).then_inc(x_in[i], 16)
            sp.wait_ge(pad_zero, 1)
            sp.dma_start(xs[0:REST, T - 1, :], x[(T - 1) * P:N, :]).then_inc(x_in[-1], 16)
            sp.dma_start(W[:, :, :], a["W"].rearrange("(k p) n -> p k n", p=P)).then_inc(weights_in, 16)
            sp.dma_start(Wr[:, :, :], a["Wr"].rearrange("(k p) n -> p k n", p=P)).then_inc(weights_in, 16)
            sp.dma_start(br[:, :], a["br"].rearrange("(o n) -> o n", o=1)).then_inc(weights_in, 16)
            for buf, name in ((bias_bc, "b"), (slope_bc, "prelu_a"), (gamma_bc, "gamma"), (beta_bc, "beta")):
                sp.dma_start(buf[:, :], a[name].rearrange("(o n) -> o n", o=1).to_broadcast([P, D])).then_inc(weights_in, 16)

            for i in range(7):
                lo, hi = T // 7 * i, T // 7 * (i + 1)
                sp.wait_ge(h_scaled, hi)
                sp.dma_start(h_table[lo * P:hi * P, :].rearrange("(t p) d -> p t d", p=P), hs[:, lo:hi, :]).then_inc(h_stored, 16)

            sp.wait_ge(table_ready, 1)
            with sp.Fori(0, T) as d:
                start, n, first = block_edges(sp, d)
                with sp.Fori(0, n) as j:
                    b = first + j
                    at = nc.s_assert_within(start + j * BATCH, 0, EDGES, skip_runtime_bounds_check_because="a block's last batch starts before its last edge")

                    def edges(t, lo, hi):
                        return t[ds(at, BATCH)].rearrange("(p u) -> p u", u=U)[:, lo:hi]

                    for h, (lo, hi) in enumerate(PARTS):
                        sp.wait_ge(slot_free, b * U + hi)
                        sp.dma_start(src_ix[h][:, :], edges(src, lo, hi)).then_inc(src_in[h], 16)
                        if h == 0:
                            sp.wait_ge(dst_free, b + 1)
                            sp.dma_start(dst_ix[:, :], edges(dst, 0, U)).then_inc(dst_in, 16)

            sp.wait_ge(rt, ROUTE_IX)
            for k in range(TOP_K):
                e = sp.value_load(route_ix[0:1, k:k + 1], min_val=0, max_val=NX - 1)
                sp.dma_start(W1e[:, k, :, :], a["W1"][ds(e, 1), :, :].rearrange("e (k p) f -> p (e k) f", p=P)).then_inc(experts_in, 16)
                sp.dma_start(W2e[:, k, :, :], a["W2"][ds(e, 1), :, :].rearrange("e (k p) d -> p (e k) d", p=P)).then_inc(experts_in, 16)
                with nc.allow_non_contiguous_dma(reason="512 biases, once"):
                    sp.dma_start(b1e[:, k, :], a["b1"][ds(e, 1), :].rearrange("e (k p) -> p (e k)", p=P)).then_inc(experts_in, 16)
                sp.dma_start(b2e[:, k, :], a["b2"][ds(e, 1), :].to_broadcast([P, D])).then_inc(experts_in, 16)

            with sp.Fori(0, (T - 1) // 2) as i:
                for k in range(2):
                    sp.wait_ge(fin, (i * 2 + (k + 3)) * FIN)
                    sp.dma_start(out[ds((i * 2 + k) * P, P), :], res[:, k, :]).then_inc(res_stored[k], 16)
            sp.wait_ge(fin, FIN * (T + 2))
            sp.dma_start(out[(T - 1) * P:N, :], res[0:REST, 0, :]).then_inc(res_stored[0], 16)
            sp.wait_ge(res_stored[0], 16 * (T // 2 + 1))
            sp.wait_ge(res_stored[1], 16 * (T // 2))

        @block.gpsimd
        def _(pool):
            g = nc.gpsimd
            for buf, pattern, m in ((iota, [[1, P]], 0), (block_node, [[P, T]], 0),
                                    (gpos, [[RANGE, NRANGE]], COLS), (batch_starts, [[BATCH, MAXB]], 0)):
                g.iota(buf[:, :], pattern, base=0, channel_multiplier=m, allow_small_or_imprecise_dtypes=True).then_inc(consts, 1)
            for buf, value in ((ident, 0.0), (ones, 1.0), (zero, 0.0), (valid, 1.0), (before, 1.0), (eps, LN_EPS), (neg_half, -0.5)):
                g.memset(buf[:, :], value).then_inc(consts, 1)
            pool.wait_ge(consts, CONSTS - 3)
            g.affine_select(out=ident[:, :], in_=ident[:, :], compare_op=ALU.not_equal, fill=1.0, base=0,
                            pattern=[[-1, P]], channel_multiplier=1).then_inc(consts, 1)
            g.affine_select(out=before[:, :], in_=before[:, :], compare_op=ALU.is_gt, fill=0.0, base=0,
                            pattern=[[1, T]], channel_multiplier=-1).then_inc(consts, 1)
            g.affine_select(out=valid[:, T - 1:T], in_=valid[:, T - 1:T], compare_op=ALU.is_gt, fill=0.0, base=REST,
                            pattern=[[0, 1]], channel_multiplier=-1).then_inc(consts, 1)

            pool.wait_ge(table_ready, 1)
            pool.wait_ge(h_stored, 16 * 7)
            with pool.Fori(0, T) as d:
                _, n, first = block_edges(pool, d)
                with pool.Fori(0, n) as j:
                    b = first + j
                    for h, (lo, hi) in enumerate(PARTS):
                        pool.wait_ge(src_in[h], (b + 1) * 16)
                        for u in range(lo, hi):
                            hold(pool, slot_free, b * U + (u + 1))
                            g.indirect_dma_start(
                                out=rows[:, u, :], out_offset=None, in_=h_table,
                                in_offset=bass.IndirectOffsetOnAxis(ap=src_ix[h][:, u - lo:u - lo + 1], axis=0),
                                bounds_check=T * P - 1).then_inc(rows_in[u], 16)

            with pool.Fori(0, T) as t:
                pool.wait_ge(fin, (t + 2) * FIN + 5)
                g.tensor_tensor(rstd[:, ds(t, 1)], sd[:, ds(t, 1)], neg_half[:, :], ALU.pow).then_inc(pow_ready, 1)

        @block.vector
        def _(dve):
            v = nc.vector
            pro = [0]

            def step(ins):
                pro[0] += 1
                ins.then_inc(dve_pro, 1)

            def settled():
                dve.wait_ge(dve_pro, pro[0])

            v.memset(xs[REST // 32 * 32:P, T - 1, :], 0.0).then_inc(pad_zero, 1)
            dve.sem_inc(dst_free, 1)
            dve.sem_inc(onehot_ready, U)
            dve.sem_inc(fin, 2 * FIN)
            for i, (lo, hi) in enumerate(x_parts + [(T - 1, T)]):
                dve.wait_ge(x_in[i], 16)
                for t in range(lo, hi):
                    if pro[0]:
                        settled()
                    step(v.bn_stats(stats[:, :], xs[:, t, :]))
                    settled()
                    step(v.bn_aggr(mv[:, t, :], stats[:, :]))
            dve.wait_ge(sd_made, 1)
            step(v.reciprocal(rstd[:, :], sd[:, :]))
            settled()

            def normalise(t, k):
                dve.wait_ge(xn_turned, t + 1)
                v.tensor_scalar(xn[:, k, :], tile(xs, t), mv[:, ds(t, 1), 0], rstd[:, ds(t, 1)],
                                ALU.subtract, ALU.mult).then_inc(xn_ready, 1)

            with dve.Fori(0, T // 2) as i:
                normalise(i * 2, 0)
                normalise(i * 2 + 1, 1)
            normalise(T - 1, 0)

            dve.wait_ge(edges_in, 16)
            dve.wait_ge(consts, CONSTS)
            step(v.tensor_scalar(low_i, dst_all, P - 1, None, ALU.bitwise_and))
            step(v.tensor_scalar(high_i, dst_all, P.bit_length() - 1, None, ALU.logical_shift_right))
            step(v.tensor_reduce(gmin[:, :], dst_all.rearrange("p (g c) -> p g c", c=RANGE), AXX, ALU.min))
            step(v.tensor_reduce(gmax[:, :], dst_all.rearrange("p (g c) -> p g c", c=RANGE), AXX, ALU.max))
            settled()
            step(v.tensor_copy(low, low_i))
            step(v.tensor_copy(high, high_i))
            settled()

            def hist(c, k):
                dve.wait_ge(hot_used, c + 1)
                for hot, val, n in ((hot_low, low, P), (hot_high, high, T)):
                    v.tensor_tensor(hot[:, k], iota[:, 0:n].rearrange("p (o n) -> p o n", o=1).to_broadcast([P, HB, n]),
                                    val[:, ds(c * HB, HB)].rearrange("p (c o) -> p c o", o=1).to_broadcast([P, HB, n]),
                                    ALU.is_equal).then_inc(hot_ready, 1)

            with dve.Fori(0, STEPS // 2) as i:
                hist(i * 2, 0)
                hist(i * 2 + 1, 1)

            shape = [P, T, NRANGE]

            def over_blocks(r):
                return r[:, :].rearrange("p (o g) -> p o g", o=1).to_broadcast(shape)

            node_b = block_node[:, :].rearrange("p (t o) -> p t o", o=1).to_broadcast(shape)
            step(v.tensor_tensor(hit, over_blocks(gmax), node_b, ALU.is_ge))
            step(v.tensor_tensor(cand, node_b, over_blocks(gmin), ALU.subtract))
            settled()
            step(v.scalar_tensor_tensor(out=hit, in0=cand, scalar=float(1 - P), in1=hit, op0=ALU.is_ge, op1=ALU.mult))
            settled()
            step(v.scalar_tensor_tensor(out=cand, in0=over_blocks(gpos), scalar=-BIG, in1=hit, op0=ALU.add, op1=ALU.mult))
            settled()
            step(v.tensor_reduce(lim[:, 0, :], cand, AXX, ALU.min))
            settled()
            step(v.scalar_tensor_tensor(out=cand, in0=over_blocks(gpos), scalar=float(RANGE), in1=hit, op0=ALU.add, op1=ALU.mult))
            settled()
            step(v.tensor_reduce(lim[:, 1, :], cand, AXX, ALU.max))
            assert pro[0] == LIM
            dve.wait_ge(lim_turned, 1)
            step(v.tensor_reduce(span[:, 0:1], lim_ps[0][0:T, 0:P], AXX, ALU.min))
            step(v.tensor_reduce(span[:, 1:2], lim_ps[1][0:T, 0:P], AXX, ALU.max))
            settled()
            step(v.scalar_tensor_tensor(out=span[:, 0:1], in0=span[:, 0:1], scalar=BIG, in1=span[:, 1:2], op0=ALU.add, op1=ALU.min))
            settled()
            step(v.tensor_tensor(span[:, 2:3], span[:, 1:2], span[:, 0:1], ALU.subtract))
            settled()
            step(v.tensor_scalar(over[:, :], batch_starts[:, :], span[:, 2:3], None, ALU.is_lt, ALU.add, accum_out=span[:, 3:4]))
            settled()
            step(v.tensor_scalar(span[:, 3:4], span[:, 3:4], 1.0, None, ALU.max))
            assert pro[0] == SPAN
            dve.wait_ge(table_made, 1)
            for k in range(3):
                step(v.tensor_copy(table[0:1, k, :], table_ps[k]))
            settled()
            dve.sem_inc(table_ready, 1)
            dve.wait_ge(sd_made, 2)
            step(v.reciprocal(dinv[:, :], sd[:, :]))
            assert pro[0] == DINV
            settled()

            dve.wait_ge(weights_in, N_WEIGHTS)
            with dve.Fori(0, T) as d:
                _, n, first = block_edges(dve, d)
                with dve.Fori(0, n) as j:
                    b = first + j
                    dve.wait_ge(dst_in, (b + 1) * 16)
                    dve.wait_ge(onehot_ready, (b + 1) * U)
                    v.tensor_scalar(dst_loc[:, :], dst_ix[:, :], block_node[:, ds(d, 1)], None, ALU.subtract).then_inc(loc_ready, 1)
                    dve.wait_ge(loc_ready, b + 1)
                    dve.sem_inc(dst_free, 1)
                    for u in range(U):
                        dve.wait_ge(slot_free, b * U + (u + 1))
                        v.tensor_scalar(onehot[:, u, :], iota[:, :], dst_loc[:, u:u + 1], None, ALU.is_equal).then_inc(onehot_ready, 1)
                e = d * EPI
                dve.wait_ge(slot_free, (first + n + 1) * U)
                v.scalar_tensor_tensor(out=agg[:, :], in0=acc[:, 0:D], scalar=dinv[:, ds(d, 1)], in1=bias_bc[:, :],
                                       op0=ALU.mult, op1=ALU.add).then_inc(epi, 1)
                dve.wait_ge(epi, e + 1)
                v.scalar_tensor_tensor(out=neg[:, :], in0=agg[:, :], scalar=0.0, in1=slope_bc[:, :], op0=ALU.min, op1=ALU.mult).then_inc(epi, 1)
                dve.wait_ge(epi, e + 2)
                v.scalar_tensor_tensor(out=agg[:, :], in0=agg[:, :], scalar=0.0, in1=neg[:, :], op0=ALU.max, op1=ALU.add).then_inc(epi, 1)
                dve.wait_ge(epi, e + 3)
                v.tensor_tensor(tile(xs, d), tile(xs, d), agg[:, :], ALU.add).then_inc(epi, 1)
                hold(dve, epi, e + 4)
                v.bn_stats(stats[:, :], tile(xs, d)).then_inc(epi, 1)
                hold(dve, epi, e + 5)
                v.bn_aggr(mv[:, 0, :], stats[:, :]).then_inc(epi, 1)
                dve.wait_ge(sd2_made, d + 1)
                v.reciprocal(rstd[:, 0:1], sd[:, 0:1]).then_inc(epi, 1)
                dve.wait_ge(epi, e + 7)
                dve.wait_ge(z_turned, d + 1)
                dve.wait_ge(z_kept, d + 1)
                v.tensor_scalar(zst[:, :], tile(xs, d), mv[:, 0, 0:1], rstd[:, 0:1], ALU.subtract, ALU.mult).then_inc(epi, 1)

            rs = [0]

            def rstep(ins):
                rs[0] += 1
                ins.then_inc(rt, 1)

            def rsettled():
                dve.wait_ge(rt, rs[0])

            def row(i, n=NX):
                return route[0:1, i, 0:n]

            def softmax(out_row, in_row, n, acts):
                rstep(v.tensor_reduce(row(8, 1), in_row, AXX, ALU.max))
                rsettled()
                rstep(v.tensor_scalar(row(9, n), in_row, row(8, 1), None, ALU.subtract))
                dve.wait_ge(rt_act, acts)
                rstep(v.tensor_reduce(row(8, 1), row(10, n), AXX, ALU.add))
                rsettled()
                rstep(v.reciprocal(row(8, 1), row(8, 1)))
                rsettled()
                rstep(v.tensor_scalar(out_row, row(10, n), row(8, 1), None, ALU.mult))
                rsettled()

            dve.wait_ge(zsum_ready, 1)
            rstep(v.tensor_scalar(zmean[:, :], zsum[:, 0:KD], 1.0 / N, None, ALU.mult))
            dve.wait_ge(rt_pe, 1)
            rstep(v.tensor_tensor(row(0), rt_ps[0:1, 0:NX], br[:, :], ALU.add))
            rsettled()
            softmax(row(1), row(0), NX, 1)
            rstep(v.tensor_scalar(row(2), row(1), float(N), None, ALU.mult))
            rsettled()
            rstep(v.reciprocal(row(3), row(2)))
            rsettled()
            rstep(v.tensor_scalar(row(4), row(3), CAP, 1.0, ALU.mult, ALU.min))
            rsettled()
            rstep(v.tensor_tensor(row(5), row(1), row(4), ALU.mult))
            rsettled()
            softmax(row(6), row(5), NX, 2)
            rstep(v.max(row(7), row(6)))
            rsettled()
            rstep(v.max_index(route_ix[:, :], row(7), row(6)))
            assert rs[0] == ROUTE_IX
            softmax(row(11, TOP_K), row(7, TOP_K), TOP_K, 3)
            assert rs[0] == ROUTE_W
            dve.wait_ge(rt_pe, 2)
            rstep(v.tensor_copy(wts[:, :], rt_ps[:, 64:64 + TOP_K]))
            rsettled()
            dve.wait_ge(experts_in, 16 * 4 * TOP_K)
            for k in range(TOP_K):
                w2k = W2e[:, k, :, :].rearrange("p k d -> p (k d)")
                rstep(v.tensor_scalar(w2k, w2k, wts[:, k:k + 1], None, ALU.mult))
            rstep(v.tensor_scalar(b2w[:, :], b2e[:, 0, :], wts[:, 0:1], None, ALU.mult))
            assert rs[0] == ROUTE_END
            rsettled()
            for k in range(1, TOP_K):
                rstep(v.scalar_tensor_tensor(out=b2w[:, :], in0=b2e[:, k, :], scalar=wts[:, k:k + 1], in1=b2w[:, :],
                                             op0=ALU.mult, op1=ALU.add))
                rsettled()

            def finish(t, k, reused):
                f = (t + 2) * FIN
                dve.wait_ge(y_made, t + (Y_SLOTS + 1))
                v.tensor_tensor(agg[:, :], y_ps[k][:, 0:D], tile(hs, t), ALU.add).then_inc(fin, 1)
                dve.wait_ge(fin, f + 1)
                v.tensor_tensor(agg[:, :], agg[:, :], b2w[:, :], ALU.add).then_inc(fin, 1)
                dve.wait_ge(fin, f + 2)
                v.bn_stats(stats[:, :], agg[:, :]).then_inc(fin, 1)
                hold(dve, fin, f + 3)
                v.bn_aggr(mv[:, 0, :], stats[:, :]).then_inc(fin, 1)
                dve.wait_ge(fin, f + 4)
                v.tensor_scalar(sd[:, ds(t, 1)], mv[:, 0, 1:2], LN_EPS, None, ALU.add).then_inc(fin, 1)
                dve.wait_ge(pow_ready, t + 1)
                v.tensor_scalar(agg[:, :], agg[:, :], mv[:, 0, 0:1], rstd[:, ds(t, 1)], ALU.subtract, ALU.mult).then_inc(fin, 1)
                dve.wait_ge(fin, f + 6)
                v.tensor_tensor(agg[:, :], agg[:, :], gamma_bc[:, :], ALU.mult).then_inc(fin, 1)
                dve.wait_ge(fin, f + 7)
                v.tensor_tensor(neg[:, :], agg[:, :], beta_bc[:, :], ALU.add).then_inc(fin, 1)
                dve.wait_ge(fin, f + 8)
                if reused is not None:
                    dve.wait_ge(res_stored[k], reused)
                v.tensor_tensor(res[:, k, :], neg[:, :], tile(xs, t), ALU.add).then_inc(fin, 1)

            finish(0, 0, None)
            finish(1, 1, None)
            with dve.Fori(1, T // 2) as i:
                finish(i * 2, 0, i * 16)
                finish(i * 2 + 1, 1, i * 16)
            finish(T - 1, 0, 16 * (T // 2))

        @block.scalar
        def _(act):
            s = nc.scalar
            act.sem_inc(h_kept, 2)
            act.sem_inc(z_kept, 1)
            act.sem_inc(h1_kept, 4)
            act.wait_ge(consts, CONSTS)
            act.wait_ge(dve_pro, STATS)
            s.activation(sd[:, :], mv[:, :, 1], ACT.Sqrt, bias=eps[:, :]).then_inc(sd_made, 1)

            def keep_xnT(t, k):
                act.wait_ge(xn_turned, t + 3)
                s.copy(xnT[:, k, :], turn_ps[k][:, 0:D]).then_inc(xnT_ready, 1)

            def keep_h(t, k):
                act.wait_ge(h_made, t + 1)
                s.copy(tile(hs, t), h_ps[k][:, 0:D]).then_inc(h_kept, 1)

            keep_xnT(0, 0)
            with act.Fori(0, T // 2) as i:
                keep_xnT(i * 2 + 1, 1)
                keep_h(i * 2, 0)
                keep_xnT(i * 2 + 2, 0)
                keep_h(i * 2 + 1, 1)
            keep_h(T - 1, 0)

            act.wait_ge(deg_ready, 1)
            s.activation(sd[:, :], deg[:, 0:T], ACT.Sqrt, bias=ones[:, 0:1]).then_inc(sd_made, 1)
            act.wait_ge(dve_pro, DINV)
            act.wait_ge(h_kept, T + 2)
            with act.Fori(0, T) as t:
                s.activation(tile(hs, t), tile(hs, t), ACT.Copy, scale=dinv[:, ds(t, 1)]).then_inc(h_scaled, 1)

            act.wait_ge(h_stored, 16 * 7)
            with act.Fori(0, T) as d:
                act.wait_ge(epi, d * EPI + 6)
                s.activation(sd[:, 0:1], mv[:, 0, 1:2], ACT.Sqrt, bias=eps[:, :]).then_inc(sd2_made, 1)
                act.wait_ge(epi, d * EPI + 8)
                s.copy(tile(hs, d), zst[:, :])
                act.wait_ge(z_turned, d + 2)
                s.copy(zT[:, :, ds(d * P, P)], turn[:, 0:D].rearrange("p (k n) -> p k n", k=KD)).then_inc(z_kept, 1)

            for i, (at, n) in enumerate(((4, NX), (13, NX), (20, TOP_K))):
                act.wait_ge(rt, at)
                s.activation(route[0:1, 10, 0:n], route[0:1, 9, 0:n], ACT.Exp).then_inc(rt_act, 1)

            act.wait_ge(experts_in, 16 * 4 * TOP_K)

            def gelus(g, k, n):
                act.wait_ge(y_made, g * GT + GT)
                for e in range(TOP_K):
                    for f in range(KF):
                        c = e * KF + f
                        act.wait_ge(h1_made, g * (TOP_K * KF) + (c + 1))
                        s.activation(hT[:, k, e, f, 0:n], h1_ps[c % 4][:, 0:n], ACT.Gelu, bias=b1e[:, e, f:f + 1]).then_inc(h1_kept, 1)

            with act.Fori(0, NG // 2) as i:
                gelus(i * 2, 0, GT * P)
                gelus(i * 2 + 1, 1, GT * P)
            gelus(NG, 0, P)

        @block.tensor
        def _(pe):
            mm = nc.tensor.matmul
            pe.sem_inc(xn_turned, 2)
            pe.sem_inc(hot_used, 2)
            pe.sem_inc(slot_free, U)
            pe.sem_inc(z_turned, 1)
            pe.sem_inc(y_made, Y_SLOTS)
            pe.wait_ge(consts, CONSTS)
            pe.wait_ge(weights_in, N_WEIGHTS)

            def turn_x(t, k):
                pe.wait_ge(xn_ready, t + 1)
                for q in range(KD):
                    last = nc.tensor.transpose(turn_ps[k][:, q * P:(q + 1) * P], xn[:, k, q * P:(q + 1) * P], ident[:, :])
                last.then_inc(xn_turned, 1)

            def make_h(t, k):
                pe.wait_ge(xnT_ready, t + 1)
                pe.wait_ge(h_kept, t + 1)
                for q in range(KD):
                    last = mm(h_ps[k][:, 0:D], xnT[:, k, q * P:(q + 1) * P], W[:, q, :], start=(q == 0), stop=(q == KD - 1))
                last.then_inc(h_made, 1)

            turn_x(0, 0)
            with pe.Fori(0, T // 2) as i:
                turn_x(i * 2 + 1, 1)
                make_h(i * 2, 0)
                turn_x(i * 2 + 2, 0)
                make_h(i * 2 + 1, 1)
            make_h(T - 1, 0)

            mm(deg[:, 0:T], zero[:, :], zero[:, 0:T], start=True, stop=True)

            def count(c, k):
                pe.wait_ge(hot_ready, c * 2 + 2)
                for q in range(HB):
                    last = mm(deg[:, 0:T], hot_low[:, k, q, :], hot_high[:, k, q, :], start=False, stop=True, skip_group_check=True)
                last.then_inc(hot_used, 1)

            with pe.Fori(0, STEPS // 2) as i:
                count(i * 2, 0)
                count(i * 2 + 1, 1)
            pe.wait_ge(hot_used, STEPS + 2)
            pe.sem_inc(deg_ready, 1)

            pe.wait_ge(dve_pro, LIM)
            for k in range(2):
                last = nc.tensor.transpose(lim_ps[k][0:T, 0:P], lim[:, k, :], ident[:, :])
            last.then_inc(lim_turned, 1)
            pe.wait_ge(dve_pro, SPAN)
            for k, (col, mat) in enumerate(((0, ident), (3, ident), (3, before))):
                last = mm(table_ps[k], span[:, col:col + 1], mat[0:T, 0:T], start=True, stop=True)
            last.then_inc(table_made, 1)

            pe.wait_ge(table_ready, 1)
            pe.wait_ge(h_scaled, T)
            pe.wait_ge(h_kept, T + 2)
            mm(zsum[:, 0:KD], zero[:, :], zero[:, 0:KD], start=True, stop=True)
            with pe.Fori(0, T) as d:
                _, n, first = block_edges(pe, d)
                mm(acc[:, 0:D], ident[:, :], tile(hs, d), start=True, stop=True)
                with pe.Fori(0, n) as j:
                    b = first + j
                    for u in range(U):
                        pe.wait_ge(onehot_ready, b * U + (u + 1 + U))
                        pe.wait_ge(rows_in[u], (b + 1) * 16)
                        mm(acc[:, 0:D], onehot[:, u, :], rows[:, u, :], start=False, stop=True, skip_group_check=True).then_inc(slot_free, 1)
                pe.wait_ge(epi, d * EPI + 8)
                pe.wait_ge(z_kept, d + 1)
                for q in range(KD):
                    zq = zst[:, q * P:(q + 1) * P]
                    mm(zsum[:, q:q + 1], zq, valid[:, ds(d, 1)], start=False, stop=True, skip_group_check=True)
                    last = nc.tensor.transpose(turn[:, q * P:(q + 1) * P], zq, ident[:, :])
                last.then_inc(z_turned, 1)
            pe.wait_ge(z_turned, T + 1)
            pe.sem_inc(zsum_ready, 1)

            pe.wait_ge(rt, 1)
            for q in range(KD):
                last = mm(rt_ps[0:1, 0:NX], zmean[:, q:q + 1], Wr[:, q, :], start=(q == 0), stop=(q == KD - 1))
            last.then_inc(rt_pe, 1)
            pe.wait_ge(rt, ROUTE_W)
            mm(rt_ps[:, 64:64 + TOP_K], ones[0:1, :], route[0:1, 11, 0:TOP_K], start=True, stop=True).then_inc(rt_pe, 1)

            pe.wait_ge(rt, ROUTE_END)
            pe.wait_ge(z_kept, T + 1)

            def hidden(g, n):
                for e in range(TOP_K):
                    for f in range(KF):
                        c = e * KF + f
                        pe.wait_ge(h1_kept, g * (TOP_K * KF) + (c + 1))
                        for q in range(KD):
                            last = mm(h1_ps[c % 4][:, 0:n], W1e[:, e, q, f * P:(f + 1) * P], zT[:, q, ds(g * (GT * P), n)],
                                      start=(q == 0), stop=(q == KD - 1))
                        last.then_inc(h1_made, 1)

            def output(g, k, blocks):
                pe.wait_ge(h1_kept, g * (TOP_K * KF) + (TOP_K * KF + 4))
                for m in range(blocks):
                    pe.wait_ge(fin, (g * GT + m) * FIN + 1)
                    for e in range(TOP_K):
                        for f in range(KF):
                            last = mm(y_ps[(k * GT + m) % 2][:, 0:D], hT[:, k, e, f, m * P:(m + 1) * P], W2e[:, e, f, :],
                                      start=(e + f == 0), stop=(e + f == TOP_K + KF - 2))
                    last.then_inc(y_made, 1)

            hidden(0, GT * P)
            with pe.Fori(0, NG // 2 - 1) as i:
                for k in range(2):
                    hidden(i * 2 + (k + 1), GT * P)
                    output(i * 2 + k, k, GT)
            hidden(NG - 1, GT * P)
            output(NG - 2, 0, GT)
            hidden(NG, P)
            output(NG - 1, 1, GT)
            output(NG, 0, 1)


INPUTS = {"x": "x", "src": "src", "dst": "dst", "L0_gnn_W": "W", "L0_gnn_b": "b", "L0_gnn_prelu_a": "prelu_a",
          "L0_ffn_Wr": "Wr", "L0_ffn_br": "br", "L0_ffn_W1": "W1", "L0_ffn_b1": "b1", "L0_ffn_W2": "W2",
          "L0_ffn_b2": "b2", "L0_ffn_gamma": "gamma", "L0_ffn_beta": "beta"}


def kernel(**inputs):
    import numpy as np
    import concourse.bacc as bacc
    from concourse.bass_utils import run_bass_kernel_spmd

    nc = bacc.Bacc("TRN2", target_bir_lowering=False, num_devices=1)
    arrays, args = {}, {}
    n_edges = inputs["src"].shape[0]
    n_blocks = -(-inputs["x"].shape[0] // P)
    for name, short in INPUTS.items():
        v = np.ascontiguousarray(inputs[name])
        if short in ("src", "dst"):
            nowhere = 0 if short == "src" else n_blocks * P
            v = np.pad(v, (0, padded_edges(n_edges) - n_edges), constant_values=nowhere)
        arrays[f"in_{short}"] = v
        args[short] = nc.dram_tensor(f"in_{short}", v.shape, mybir.dt.from_np(v.dtype), kind="ExternalInput").ap()
    out = nc.dram_tensor("out_0", inputs["x"].shape, F32, kind="ExternalOutput").ap()
    gnn_ffn_kernel(nc, args, out, n_edges)
    r = run_bass_kernel_spmd(nc, [arrays], core_ids=[0])
    return r.results[0]["out_0"]
```

```python
from contextlib import ExitStack

import concourse.bass as bass
from concourse import mybir

ALU = mybir.AluOpType
ACT = mybir.ActivationFunctionType
AXX = mybir.AxisListType.X
F32 = mybir.dt.float32
F32R = mybir.dt.float32r
BF16 = mybir.dt.bfloat16
I32 = mybir.dt.int32
U32 = mybir.dt.uint32
ds = bass.ds

P = 128
LN_EPS = 1e-5
CAPACITY_FACTOR = 1.25
TOP_K = 2

GN = 4
GROUPS = P // GN
CPG = 2
CHUNKS = GROUPS * CPG
SC = 16
STEPS = CHUNKS // SC
BPS = SC // CPG // 2

U = 9
PARTS = ((0, 3), (3, 6), (6, 9))
RANGE = 48


def edge_columns(E):
    unit = 2 * RANGE
    return -(-(-(-E // P)) // unit) * unit


def padded_edges(E):
    return P * edge_columns(E) + max(P * U, edge_columns(E))


def gnn_ffn_kernel(nc, a, out, E):
    x, src, dst, pairs = a["x"], a["src"], a["dst"], a["pairs"]
    N, D = out.shape
    NX, _, F = a["W1"].shape
    T = -(-N // P)
    REST = N - (T - 1) * P
    KD, KF = D // P, F // P
    COLS = edge_columns(E)
    EDGES = P * COLS
    KEYS = GN * T
    HSTEPS = COLS // SC
    H_MAIN = 4 * (T // 2)
    H_FIRST = HSTEPS - H_MAIN
    NRANGE = COLS // RANGE
    BATCH = P * U
    MAXB = -(-EDGES // BATCH) + 1
    BIG = float(EDGES)
    CAP = float(-(-N * CAPACITY_FACTOR // NX))
    GT = 3
    NG = (T - 1) // GT
    CF = TOP_K * KF
    assert T % 2 == 1 and T == NG * GT + 1 and NG % 2 == 0
    assert H_FIRST > 0 and H_FIRST % 2 == 0 and STEPS % 2 == 0 and CPG == 2 and 2 * KEYS <= 512 and KEYS <= 256

    x1_dram = nc.dram_tensor("x1_dram", (T * P, D), F32, kind="Internal").ap()
    starts_dram = nc.dram_tensor("starts_dram", (T, GROUPS), I32, kind="Internal").ap()
    h_table = nc.dram_tensor("h_table", (T * P, 2 * D), F32, kind="Internal").ap()

    with ExitStack() as ctx:
        def sb(name, shape, dt=F32):
            return ctx.enter_context(nc.sbuf_tensor(name, shape, dt))

        def sem(name):
            return ctx.enter_context(nc.semaphore(name))

        ident = sb("ident", [P, P])
        ident_r = sb("ident_r", [P, P], F32R)
        iota = sb("iota", [P, P])
        iota16 = sb("iota16", [P, KEYS, SC], BF16)
        ones = sb("ones", [P, P])
        zero = sb("zero", [P, P])
        valid = sb("valid", [P, T + 2])
        dinv = sb("dinv", [P, T])
        eps = sb("eps", [P, 1])
        neg_half = sb("neg_half", [P, 1])
        bias_bc = sb("bias_bc", [P, D])
        slope_bc = sb("slope_bc", [P, D])
        gamma_bc = sb("gamma_bc", [P, D])
        beta_bc = sb("beta_bc", [P, D])
        W = sb("W", [P, KD, D])
        Wr = sb("Wr", [P, KD, NX])
        br = sb("br", [1, NX])
        below = sb("below", [P, GROUPS + 1])
        before = sb("before", [T, T])
        block_key = sb("block_key", [P, T])
        group_key = sb("group_key", [P, GROUPS, CPG])
        unsorted = sb("unsorted", [P, 1])
        deg_sb = sb("deg_sb", [P, T])
        cum = sb("cum", [T, GROUPS + 1])
        total = sb("total", [T, GROUPS + 1])
        width = sb("width", [T, GROUPS])
        crowded = sb("crowded", [T, 1])
        starts = sb("starts", [T, GROUPS + 1], I32)
        flag = sb("flag", [1, 1], I32)
        starts_row = sb("starts_row", [1, T * GROUPS], I32)

        hot_src = sb("hot_src", [P, 2, P, SC], BF16)
        hot_key = sb("hot_key", [P, 2, KEYS, SC], BF16)
        raw = sb("raw", [P, 2, CHUNKS, 2], I32)
        blk_i = sb("blk_i", [P, CHUNKS], I32)
        wide = sb("wide", [P, CHUNKS])
        place = sb("place", [P, 2, CHUNKS], BF16)
        key = sb("key", [P, 2, CHUNKS], BF16)

        mv = sb("mv", [P, T, 2])
        mvb = sb("mvb", [P, 2])
        mean = sb("mean", [P, T])
        sd = sb("sd", [P, T])
        rstd = sb("rstd", [P, T])
        shift = sb("shift", [P, T])
        stats = sb("stats", [P, T, 6])
        xin = sb("xin", [P, 2, D])
        x1 = sb("x1", [P, 2, D])
        zst = sb("zst", [P, 2, D])
        low = sb("low", [P, D])
        agg = sb("agg", [P, D])
        neg = sb("neg", [P, D])

        route = sb("route", [1, 12, NX])
        route_ix = sb("route_ix", [1, 8], U32)
        zmean = sb("zmean", [P, KD])
        wts = sb("wts", [P, TOP_K])
        b1e = sb("b1e", [P, TOP_K, KF])

        WORD = 4
        TAB_AT = nc.sbuf_usable_end - (T * 2 * D + 2 * P * T) * WORD
        TAB_AT -= TAB_AT % 64
        ADJ_AT = TAB_AT + T * 2 * D * WORD
        REGION_END = ADJ_AT + 2 * P * T * WORD
        assert nc.sbuf_base <= TAB_AT, (nc.sbuf_base, TAB_AT)

        def tenants(at, end=REGION_END):
            place_at = [at]

            def take(name, shape, dt=F32):
                size = 2 if dt == BF16 else WORD
                for n in shape[1:]:
                    size *= n
                t = nc.alloc_sbuf_tensor_at(name, shape, dt, offset=place_at[0])
                place_at[0] += -(-size // 64) * 64
                assert place_at[0] <= end
                return t
            return take

        tab = tenants(TAB_AT)("tab", [P, T, 2 * D], F32R)
        room = tenants(ADJ_AT)
        adj = [room(f"adj{k}", [P, P * T], F32R) for k in range(2)]
        room = tenants(TAB_AT, ADJ_AT)
        xs = room("xs", [P, T, D])
        xn = room("xn", [P, 2, D])
        xnT = room("xnT", [P, 2, D])
        dst_all = room("dst_all", [P, COLS + 1], I32)
        low_i = room("low_i", [P, COLS], I32)
        high_i = room("high_i", [P, COLS], I32)
        low7 = room("low7", [P, COLS], BF16)
        high = room("high", [P, COLS], BF16)
        falls = room("falls", [P, COLS])
        hs = tenants(ADJ_AT)("hs", [P, T, D])
        room = tenants(ADJ_AT)
        rows = room("rows", [P, U, 2 * D])
        onehot = room("onehot", [P, U, P])
        dst_gen = room("dst_gen", [P, COLS], I32)
        hit = room("hit", [P, T, NRANGE])
        cand = room("cand", [P, T, NRANGE])
        gmin, gmax, gpos = (room(n, [P, NRANGE]) for n in ("gmin", "gmax", "gpos"))
        lim = room("lim", [P, 2, T])
        span = room("span", [T, 4])
        batch_starts = room("batch_starts", [T, MAXB])
        over = room("over", [T, MAXB])
        block_node = room("block_node", [P, T])
        table = room("table", [1, 3, T], I32)
        src_ix = [room(f"src_ix{h}", [P, hi - lo], I32) for h, (lo, hi) in enumerate(PARTS)]
        dst_ix = room("dst_ix", [P, U], I32)
        dst_loc = room("dst_loc", [P, U])
        room = tenants(TAB_AT)
        W1e = room("W1e", [P, TOP_K, KD, F])
        W2e = room("W2e", [P, TOP_K, KF, D])
        W1h, W1l = (room(n, [P, TOP_K, KD, F], F32R) for n in ("W1h", "W1l"))
        W2h, W2l = (room(n, [P, TOP_K, KF, D], F32R) for n in ("W2h", "W2l"))
        zTh, zTl = (room(n, [P, 2, KD, GT * P], F32R) for n in ("zTh", "zTl"))
        gh, gl = (room(n, [P, 2, CF, GT * P], F32R) for n in ("gh", "gl"))
        gf = room("gf", [P, 2, GT * P])
        x1f, zf, zb, x1b = (room(n, [P, 2, GT, D]) for n in ("x1f", "zf", "zb", "x1b"))
        pre = room("pre", [P, GT, D])
        res = room("res", [P, 2, D])
        b2e = room("b2e", [P, TOP_K, D])
        b2w = room("b2w", [P, D])
        stf = room("stf", [P, GT, 6])
        mvf = room("mvf", [P, GT, 2])
        vare = room("vare", [P, T])
        rstdf = room("rstdf", [P, T])

        banks = [ctx.enter_context(nc.psum_tensor(f"bank{i}", [P, 512], F32)) for i in range(8)]
        h_ps, turn_ps, deg = banks[0:2], banks[2:4], banks[4]
        cum_ps, off_ps, flag_ps = banks[5], banks[6], banks[7]
        adj_ps, acc, zsum, rt_ps = banks[0:BPS], banks[4:6], banks[6], banks[7]
        lim_ps = banks[0:2]
        table_ps = [banks[2][0:1, 128 * k:128 * k + T] for k in range(3)]
        zt_ps, h1_ps, y_ps = banks[0:2], banks[2:6], banks[6:8]

        held = sem("held")
        consts = sem("consts")
        x_parts = [(0, 12), (12, 24), (24, 36), (36, T)]
        x_in = [sem(f"x_in{i}") for i in range(len(x_parts))]
        edges_in = sem("edges_in")
        weights_in = sem("weights_in")
        dve_pro = sem("dve_pro")
        sd_made = sem("sd_made")
        xn_ready = sem("xn_ready")
        xn_turned = sem("xn_turned")
        xnT_ready = sem("xnT_ready")
        h_made = sem("h_made")
        h_kept = sem("h_kept")
        ones_ready = sem("ones_ready")
        counted = sem("counted")
        deg_ready = sem("deg_ready")
        cum_made = sem("cum_made")
        off_made = sem("off_made")
        flag_ready = sem("flag_ready")
        starts_out = sem("starts_out")
        starts_in = sem("starts_in")
        hi_made = sem("hi_made")
        lo_made = sem("lo_made")
        raw_in = [sem(f"raw_in{k}") for k in range(2)]
        raw_free = sem("raw_free")
        decoded = sem("decoded")
        hot_ready = sem("hot_ready")
        bank_ready = sem("bank_ready")
        bank_kept = sem("bank_kept")
        acc_ready = sem("acc_ready")
        low_kept = sem("low_kept")
        epi = sem("epi")
        sd2_made = sem("sd2_made")
        tile_in = [sem(f"tile_in{k}") for k in range(2)]
        x1_stored = [sem(f"x1_stored{k}") for k in range(2)]
        x1_out = sem("x1_out")
        zsum_done = sem("zsum_done")
        g_dst_in = sem("g_dst_in")
        g_consts = sem("g_consts")
        g_pro = sem("g_pro")
        h_stored = sem("h_stored")
        lim_turned = sem("lim_turned")
        table_made = sem("table_made")
        table_ready = sem("table_ready")
        src_in = [sem(f"src_in{h}") for h in range(len(PARTS))]
        dst_in = sem("dst_in")
        dst_free = sem("dst_free")
        rows_in = [sem(f"rows_in{u}") for u in range(U)]
        loc_ready = sem("loc_ready")
        onehot_ready = sem("onehot_ready")
        slot_free = sem("slot_free")
        zsum_ready = sem("zsum_ready")
        rt = sem("rt")
        rt_pe = sem("rt_pe")
        rt_act = sem("rt_act")
        experts_in = sem("experts_in")
        w1_split = sem("w1_split")
        x1_in = [sem(f"x1_in{k}") for k in range(2)]
        shift_ready = sem("shift_ready")
        z_made = sem("z_made")
        prep = sem("prep")
        z_turned = sem("z_turned")
        zh_kept = sem("zh_kept")
        zl_kept = sem("zl_kept")
        h1_made = sem("h1_made")
        g_made = sem("g_made")
        gl_made = sem("gl_made")
        y_made = sem("y_made")
        norm = sem("norm")
        pow_ready = sem("pow_ready")
        done = sem("done")
        res_stored = sem("res_stored")
        res_free = sem("res_free")

        N_CONSTS = 16
        N_WEIGHTS = 16 * 7
        EPI = 9
        NORM = 4
        PREP = 2
        ROUTE_IX, ROUTE_W, ROUTE_END = 18, 23, 31

        SORTED = 6
        STATS = SORTED + 2 * T
        RSTD = STATS + 2
        DEG = RSTD + 1
        DINV = DEG + 1
        CUM = DINV + 4
        STARTS = CUM + 1
        G_LIM, G_SPAN = 9, 15

        block = ctx.enter_context(nc.Block())

        def hold(eng, semaphore, value):
            eng.wait_ge(semaphore, value)
            eng.sem_inc(held, 1)

        def tile(buf, t):
            return buf[:, ds(t, 1), :].rearrange("p o d -> p (o d)")

        def is_dense(eng):
            eng.wait_ge(flag_ready, 1)
            return eng.value_load(flag[0:1, 0:1], min_val=0, max_val=EDGES + T * GROUPS) == 0

        def block_edges(eng, d):
            return (eng.value_load(table[0:1, 0, ds(d, 1)], min_val=0, max_val=EDGES),
                    eng.value_load(table[0:1, 1, ds(d, 1)], min_val=1, max_val=MAXB),
                    eng.value_load(table[0:1, 2, ds(d, 1)], min_val=0, max_val=MAXB * T))

        @block.sync
        def _(sp):
            sp.sem_inc(res_free, 2)
            sp.dma_start(dst_all[:, 0:COLS], dst[0:EDGES].rearrange("(p c) -> p c", p=P)).then_inc(edges_in, 16)
            with nc.allow_non_contiguous_dma(reason="the edge after each partition's last, once"):
                sp.dma_start(dst_all[:, COLS:COLS + 1], dst[COLS:COLS + EDGES].rearrange("(p c) -> p c", p=P)[:, 0:1]).then_inc(edges_in, 16)
            for i, (lo, hi) in enumerate(x_parts):
                sp.dma_start(xs[:, lo:hi, :], x[lo * P:hi * P, :].rearrange("(t p) d -> p t d", p=P)).then_inc(x_in[i], 16)
            sp.dma_start(W[:, :, :], a["W"].rearrange("(k p) n -> p k n", p=P)).then_inc(weights_in, 16)
            sp.dma_start(Wr[:, :, :], a["Wr"].rearrange("(k p) n -> p k n", p=P)).then_inc(weights_in, 16)
            sp.dma_start(br[:, :], a["br"].rearrange("(o n) -> o n", o=1)).then_inc(weights_in, 16)
            for buf, name in ((bias_bc, "b"), (slope_bc, "prelu_a"), (gamma_bc, "gamma"), (beta_bc, "beta")):
                sp.dma_start(buf[:, :], a[name].rearrange("(o n) -> o n", o=1).to_broadcast([P, D])).then_inc(weights_in, 16)

            sp.wait_ge(dve_pro, STARTS)
            sp.dma_start(starts_dram[:, :], starts[:, 0:GROUPS]).then_inc(starts_out, 16)
            sp.wait_ge(starts_out, 16)
            sp.dma_start(starts_row[:, :], starts_dram.rearrange("(o t) g -> o (t g)", o=1)).then_inc(starts_in, 16)

            sp.wait_ge(starts_in, 16)
            with sp.If(is_dense(sp)):
                def load_edges(d, k):
                    hold(sp, raw_free, d + 1)
                    for g in range(GROUPS):
                        e = nc.s_assert_within(sp.value_load(starts_row[0:1, ds(d * GROUPS + g, 1)]), 0, EDGES,
                                               skip_runtime_bounds_check_because="counts of edges sum to at most all of them")
                        sp.dma_start(raw[:, k, g * CPG:(g + 1) * CPG, :],
                                     pairs[ds(e, P * CPG), :].rearrange("(p c) s -> p c s", c=CPG)).then_inc(raw_in[k], 16)

                with sp.Fori(0, T // 2) as i:
                    load_edges(i * 2, 0)
                    load_edges(i * 2 + 1, 1)
                load_edges(T - 1, 0)
            with sp.Else():
                sp.wait_ge(lo_made, T)
                sp.dma_start(dst_gen[:, :], dst[0:EDGES].rearrange("(p c) -> p c", p=P)).then_inc(g_dst_in, 16)
                sp.dma_start(h_table.rearrange("(t p) d -> p t d", p=P), tab[:, :, :].bitcast(F32)).then_inc(h_stored, 16)
                sp.wait_ge(table_ready, 1)
                with sp.Fori(0, T) as d:
                    start, n, first = block_edges(sp, d)
                    with sp.Fori(0, n) as j:
                        b = first + j
                        at = nc.s_assert_within(start + j * BATCH, 0, EDGES, skip_runtime_bounds_check_because="a block's last batch starts before its last edge")

                        def edges(t, lo, hi):
                            return t[ds(at, BATCH)].rearrange("(p u) -> p u", u=U)[:, lo:hi]

                        for h, (lo, hi) in enumerate(PARTS):
                            sp.wait_ge(slot_free, b * U + hi)
                            sp.dma_start(src_ix[h][:, :], edges(src, lo, hi)).then_inc(src_in[h], 16)
                            if h == 0:
                                sp.wait_ge(dst_free, b + 1)
                                sp.dma_start(dst_ix[:, :], edges(dst, 0, U)).then_inc(dst_in, 16)

            def load_x1(g, k, n):
                sp.dma_start(x1f[:, k, 0:n, :], x1_dram[ds(g * (GT * P), n * P), :].rearrange("(t p) d -> p t d", p=P)).then_inc(x1_in[k], 16)

            sp.wait_ge(x1_out, T + 2)
            load_x1(0, 0, GT)
            load_x1(1, 1, GT)
            sp.wait_ge(rt, ROUTE_IX)
            for k in range(TOP_K):
                e = sp.value_load(route_ix[0:1, k:k + 1], min_val=0, max_val=NX - 1)
                sp.dma_start(W1e[:, k, :, :], a["W1"][ds(e, 1), :, :].rearrange("e (k p) f -> p (e k) f", p=P)).then_inc(experts_in, 16)
                sp.dma_start(W2e[:, k, :, :], a["W2"][ds(e, 1), :, :].rearrange("e (k p) d -> p (e k) d", p=P)).then_inc(experts_in, 16)
                with nc.allow_non_contiguous_dma(reason="512 biases, once"):
                    sp.dma_start(b1e[:, k, :], a["b1"][ds(e, 1), :].rearrange("e (k p) -> p (e k)", p=P)).then_inc(experts_in, 16)
                sp.dma_start(b2e[:, k, :], a["b2"][ds(e, 1), :].to_broadcast([P, D])).then_inc(experts_in, 16)

            def store(t, kk, n):
                sp.wait_ge(done, t * 2 + (2 * GT * 2 + 2))
                sp.dma_start(out[ds(t * P, n), :], res[0:n, kk, :]).then_inc(res_stored, 16)
                sp.wait_ge(res_stored, t * 16 + 16)
                sp.sem_inc(res_free, 1)

            def next_group(g, k, n, ahead):
                if ahead:
                    sp.wait_ge(prep, g * PREP + 3 * PREP)
                    sp.wait_ge(z_made, g * GT + GT)
                    load_x1(g + 2, k, ahead)
                for m in range(n):
                    store(g * GT + m, (k * GT + m) % 2, P)

            with sp.Fori(0, NG // 2 - 1) as i:
                next_group(i * 2, 0, GT, GT)
                next_group(i * 2 + 1, 1, GT, GT)
            next_group(NG - 2, 0, GT, 1)
            next_group(NG - 1, 1, GT, 0)
            store(T - 1, 0, REST)

        @block.gpsimd
        def _(pool):
            g = nc.gpsimd
            pool.sem_inc(x1_out, 2)
            for buf, pattern, m in ((iota[:, :], [[1, P]], 0),
                                    (iota16[:, :, :], [[1, KEYS], [0, SC]], 0),
                                    (block_key[:, :], [[-P * T, T]], 0),
                                    (group_key[:, :, :], [[-KEYS, GROUPS], [0, CPG]], 0)):
                g.iota(buf, pattern, base=0, channel_multiplier=m, allow_small_or_imprecise_dtypes=True).then_inc(consts, 1)
            for buf, value in ((ident, 0.0), (ones, 1.0), (zero, 0.0), (valid, 1.0), (before, 1.0), (below, 1.0), (eps, LN_EPS), (neg_half, -0.5)):
                g.memset(buf[:, :], value).then_inc(consts, 1)
            pool.wait_ge(consts, N_CONSTS - 4)
            g.affine_select(out=ident[:, :], in_=ident[:, :], compare_op=ALU.not_equal, fill=1.0, base=0,
                            pattern=[[-1, P]], channel_multiplier=1).then_inc(consts, 1)
            g.affine_select(out=before[:, :], in_=before[:, :], compare_op=ALU.is_gt, fill=0.0, base=0,
                            pattern=[[1, T]], channel_multiplier=-1).then_inc(consts, 1)
            g.affine_select(out=below[:, :], in_=below[:, :], compare_op=ALU.is_gt, fill=0.0, base=0,
                            pattern=[[GN, GROUPS + 1]], channel_multiplier=-1).then_inc(consts, 1)
            g.affine_select(out=valid[:, T + 1:T + 2], in_=valid[:, T + 1:T + 2], compare_op=ALU.is_gt, fill=0.0, base=REST,
                            pattern=[[0, 1]], channel_multiplier=-1).then_inc(consts, 1)

            def load_tile(d, k):
                g.dma_start(xin[:, k, :], x[ds(d * P, P), :]).then_inc(tile_in[k], 16)

            def store_x1(d, k, stored):
                hold(pool, epi, d * EPI + (2 * EPI + 5))
                g.dma_start(x1_dram[ds(d * P, P), :], x1[:, k, :]).then_inc(x1_stored[k], 16)
                if stored is not None:
                    finish_x1(k, stored)

            def finish_x1(k, stored):
                hold(pool, x1_stored[k], stored)
                pool.sem_inc(x1_out, 1)

            with pool.If(is_dense(pool)):
                load_tile(0, 0)
                load_tile(1, 1)
                with pool.Fori(0, T // 2 - 1) as i:
                    for k in range(2):
                        store_x1(i * 2 + k, k, None)
                        load_tile(i * 2 + (k + 2), k)
                        finish_x1(k, i * 16 + 16)
                store_x1(T - 3, 0, None)
                load_tile(T - 1, 0)
                finish_x1(0, T // 2 * 16)
                store_x1(T - 2, 1, T // 2 * 16)
                store_x1(T - 1, 0, (T // 2 + 1) * 16)
            with pool.Else():
                pool.wait_ge(lo_made, T)
                for buf, pattern, m in ((gpos, [[RANGE, NRANGE]], COLS), (block_node, [[P, T]], 0), (batch_starts, [[BATCH, MAXB]], 0)):
                    g.iota(buf[:, :], pattern, base=0, channel_multiplier=m, allow_small_or_imprecise_dtypes=True).then_inc(g_consts, 1)
                pool.wait_ge(table_ready, 1)
                pool.wait_ge(h_stored, 16)
                with pool.Fori(0, T) as d:
                    load_tile(d, 0)
                    _, n, first = block_edges(pool, d)
                    with pool.Fori(0, n) as j:
                        b = first + j
                        for h, (lo, hi) in enumerate(PARTS):
                            pool.wait_ge(src_in[h], (b + 1) * 16)
                            for u in range(lo, hi):
                                hold(pool, slot_free, b * U + (u + 1))
                                g.indirect_dma_start(
                                    out=rows[:, u, :], out_offset=None, in_=h_table,
                                    in_offset=bass.IndirectOffsetOnAxis(ap=src_ix[h][:, u - lo:u - lo + 1], axis=0),
                                    bounds_check=T * P - 1).then_inc(rows_in[u], 16)
                    store_x1(d, 0, d * 16 + 16)

            pool.sem_inc(prep, 2 * PREP)

            def bc(row, n):
                return row[:, :].rearrange("p (o d) -> p o d", o=1).to_broadcast([P, n, D])

            def prepare(gr, k, n):
                hold(pool, done, gr * (2 * GT) + 2 * GT)
                hold(pool, z_made, gr * GT + n)
                g.tensor_tensor(zb[:, k, 0:n, :], zf[:, k, 0:n, :], bc(b2w, n), ALU.add).then_inc(prep, 1)
                g.tensor_tensor(x1b[:, k, 0:n, :], x1f[:, k, 0:n, :], bc(beta_bc, n), ALU.add).then_inc(prep, 1)

            def power(t):
                hold(pool, norm, t * NORM + 3 * NORM)
                g.tensor_tensor(rstdf[:, ds(t, 1)], vare[:, ds(t, 1)], neg_half[:, :], ALU.pow).then_inc(pow_ready, 1)

            pool.wait_ge(rt, ROUTE_END)
            prepare(0, 0, GT)
            prepare(1, 1, GT)
            with pool.Fori(0, NG // 2 - 1) as i:
                for k in range(2):
                    for m in range(GT):
                        power(i * (2 * GT) + (k * GT + m))
                    prepare(i * 2 + (k + 2), k, GT)
            for m in range(GT):
                power((NG - 2) * GT + m)
            prepare(NG, 0, 1)
            for t in range((NG - 1) * GT, T):
                power(t)

        @block.vector
        def _(dve):
            v = nc.vector
            pro = [0]

            def step(ins):
                pro[0] += 1
                ins.then_inc(dve_pro, 1)

            def settled():
                dve.wait_ge(dve_pro, pro[0])

            for k in range(2):
                v.memset(zst[:, k, :], 0.0).then_inc(zsum_done, 1)
            dve.sem_inc(raw_free, 2)
            dve.sem_inc(hot_ready, 2 * STEPS)
            dve.sem_inc(epi, 2 * EPI)
            dve.sem_inc(dst_free, 1)
            dve.sem_inc(onehot_ready, U)
            dve.sem_inc(zl_kept, KD)
            dve.sem_inc(gl_made, 2)
            dve.sem_inc(norm, 2 * NORM)
            dve.sem_inc(done, 4 * GT)

            dve.wait_ge(edges_in, 32)
            step(v.tensor_scalar(low_i[:, :], dst_all[:, 0:COLS], P - 1, None, ALU.bitwise_and))
            step(v.tensor_scalar(high_i[:, :], dst_all[:, 0:COLS], P.bit_length() - 1, None, ALU.logical_shift_right))
            step(v.tensor_tensor(falls[:, :], dst_all[:, 0:COLS], dst_all[:, 1:COLS + 1], ALU.is_gt))
            settled()
            step(v.tensor_copy(low7[:, :], low_i[:, :]))
            step(v.tensor_copy(high[:, :], high_i[:, :]))
            step(v.tensor_reduce(unsorted[:, :], falls[:, :], AXX, ALU.add))
            assert pro[0] == SORTED
            settled()
            dve.wait_ge(consts, N_CONSTS)
            v.tensor_copy(ident_r[:, :], ident[:, :]).then_inc(consts, 1)

            def one_hot(hot, values, n):
                return v.tensor_tensor(hot, iota16[:, 0:n, :], values.rearrange("p (o c) -> p o c", o=1).to_broadcast([P, n, SC]), ALU.is_equal)

            def degree_step(c, k):
                dve.wait_ge(counted, c + 1)
                one_hot(hot_src[:, k, :, :], low7[:, ds(c * SC, SC)], P).then_inc(ones_ready, 1)
                one_hot(hot_key[:, k, 0:T, :], high[:, ds(c * SC, SC)], T).then_inc(ones_ready, 1)

            with dve.Fori(0, H_FIRST // 2) as i:
                degree_step(i * 2, 0)
                degree_step(i * 2 + 1, 1)

            for i, (lo, hi) in enumerate(x_parts):
                dve.wait_ge(x_in[i], 16)
                for t in range(lo, hi):
                    step(v.bn_stats(stats[:, t, :], xs[:, t, :]))
                settled()
                for t in range(lo, hi):
                    step(v.bn_aggr(mv[:, t, :], stats[:, t, :]))
            assert pro[0] == STATS
            settled()
            dve.wait_ge(sd_made, 1)
            step(v.reciprocal(rstd[:, :], sd[:, :]))
            settled()
            step(v.scalar_tensor_tensor(out=shift[:, :], in0=mv[:, :, 0], scalar=-1.0, in1=rstd[:, :], op0=ALU.mult, op1=ALU.mult))
            assert pro[0] == RSTD

            with dve.Fori(0, H_MAIN // 2) as i:
                degree_step(i * 2 + H_FIRST, 0)
                degree_step(i * 2 + (H_FIRST + 1), 1)

            dve.wait_ge(deg_ready, 1)
            step(v.tensor_copy(deg_sb[:, :], deg[:, 0:T]))
            assert pro[0] == DEG
            dve.wait_ge(sd_made, 2)
            step(v.reciprocal(dinv[:, :], sd[:, :]))
            assert pro[0] == DINV
            dve.wait_ge(cum_made, 1)
            step(v.tensor_copy(cum[:, :], cum_ps[0:T, 0:GROUPS + 1]))
            settled()
            step(v.tensor_copy(total[:, :], cum[:, GROUPS:GROUPS + 1].to_broadcast([T, GROUPS + 1])))
            step(v.tensor_tensor(width[:, :], cum[:, 1:GROUPS + 1], cum[:, 0:GROUPS], ALU.subtract))
            settled()
            step(v.tensor_scalar(width[:, :], width[:, :], float(CPG * P), None, ALU.is_gt, ALU.add, accum_out=crowded[:, :]))
            assert pro[0] == CUM
            dve.wait_ge(off_made, 1)
            step(v.tensor_tensor(starts[:, :], cum[:, :], off_ps[0:T, 0:GROUPS + 1], ALU.add))
            assert pro[0] == STARTS
            v.tensor_copy(flag[:, :], flag_ps[0:1, 0:1]).then_inc(flag_ready, 1)
            with dve.Fori(0, T) as t:
                dve.wait_ge(hi_made, t + 1)
                v.scalar_tensor_tensor(out=tile(tab, t)[:, D:2 * D], in0=tile(hs, t), scalar=dinv[:, ds(t, 1)],
                                       in1=tile(tab, t)[:, 0:D].bitcast(F32), op0=ALU.mult, op1=ALU.subtract).then_inc(lo_made, 1)
            dve.wait_ge(lo_made, T)
            dve.wait_ge(weights_in, N_WEIGHTS)

            def x1_sum(d, k, alone):
                e = d * EPI + 2 * EPI
                dve.wait_ge(epi, e)
                dve.wait_ge(acc_ready, d + 1)
                dve.wait_ge(low_kept, d + 3)
                v.scalar_tensor_tensor(out=agg[:, :], in0=acc[k][:, 0:D], scalar=dinv[:, ds(d, 1)], in1=low[:, :],
                                       op0=ALU.mult, op1=ALU.add).then_inc(epi, 1)
                dve.wait_ge(epi, e + 1)
                v.tensor_tensor(agg[:, :], agg[:, :], bias_bc[:, :], ALU.add).then_inc(epi, 1)
                dve.wait_ge(epi, e + 2)
                v.scalar_tensor_tensor(out=neg[:, :], in0=agg[:, :], scalar=0.0, in1=slope_bc[:, :], op0=ALU.min, op1=ALU.mult).then_inc(epi, 1)
                dve.wait_ge(epi, e + 3)
                v.scalar_tensor_tensor(out=agg[:, :], in0=agg[:, :], scalar=0.0, in1=neg[:, :], op0=ALU.max, op1=ALU.add).then_inc(epi, 1)

            def x1_stats(d, k, alone, loaded):
                e = d * EPI + 2 * EPI
                dve.wait_ge(epi, e + 4)
                dve.wait_ge(tile_in[k], loaded)
                dve.wait_ge(x1_out, d + (1 + alone))
                v.tensor_tensor(x1[:, k, :], xin[:, k, :], agg[:, :], ALU.add).then_inc(epi, 1)
                hold(dve, epi, e + 5)
                v.bn_stats(stats[:, 0, :], x1[:, k, :]).then_inc(epi, 1)
                hold(dve, epi, e + 6)
                v.bn_aggr(mvb[:, :], stats[:, 0, :]).then_inc(epi, 1)

            def x1_norm(d, k, alone):
                e = d * EPI + 2 * EPI
                hold(dve, sd2_made, d * 2 + 2)
                v.reciprocal(rstd[:, ds(d, 1)], sd[:, 0:1]).then_inc(epi, 1)
                dve.wait_ge(epi, e + 8)
                dve.wait_ge(zsum_done, d + (3 + alone))
                v.tensor_scalar(zst[:, k, :], x1[:, k, :], mvb[:, 0:1], rstd[:, ds(d, 1)], ALU.subtract, ALU.mult).then_inc(epi, 1)

            with dve.If(is_dense(dve)):
                def decode(b, k, loaded):
                    source, target = raw[:, k, :, 0], raw[:, k, :, 1]
                    dve.wait_ge(raw_in[k], loaded)
                    dve.wait_ge(hot_ready, b * (2 * STEPS) + 2 * STEPS)
                    v.tensor_scalar(blk_i[:, :], source, P.bit_length() - 1, None, ALU.logical_shift_right).then_inc(decoded, 1)
                    dve.wait_ge(decoded, b * 4 + 1)
                    v.scalar_tensor_tensor(out=place[:, k, :], in0=blk_i[:, :], scalar=float(-P), in1=source, op0=ALU.mult, op1=ALU.add).then_inc(decoded, 1)
                    v.scalar_tensor_tensor(out=wide[:, :], in0=target, scalar=float(T), in1=blk_i[:, :], op0=ALU.mult, op1=ALU.add).then_inc(decoded, 1)
                    dve.wait_ge(decoded, b * 4 + 3)
                    dve.sem_inc(raw_free, 1)
                    v.scalar_tensor_tensor(out=key[:, k, :], in0=wide[:, :], scalar=block_key[:, ds(b, 1)],
                                           in1=group_key[:, :, :].rearrange("p g c -> p (g c)"), op0=ALU.add, op1=ALU.add).then_inc(decoded, 1)
                    dve.wait_ge(decoded, b * 4 + 4)

                def hot_step(b, k, s):
                    kk, cols = s % 2, slice(s * SC, (s + 1) * SC)
                    dve.wait_ge(bank_ready, b * (STEPS * BPS) + (s + 1) * BPS)
                    one_hot(hot_src[:, kk, :, :], place[:, k, cols], P).then_inc(hot_ready, 1)
                    one_hot(hot_key[:, kk, :, :], key[:, k, cols], KEYS).then_inc(hot_ready, 1)

                def rows_of(b, k, loaded):
                    decode(b, k, loaded)
                    for s in range(STEPS):
                        hot_step(b, k, s)

                PER = 16 * GROUPS
                rows_of(0, 0, PER)
                rows_of(1, 1, PER)

                def both(b, k, turn):
                    d = b - 2
                    decode(b, k, turn * PER + PER)
                    hot_step(b, k, 0)
                    x1_sum(d, k, 0)
                    hot_step(b, k, 1)
                    x1_stats(d, k, 0, turn * 16)
                    hot_step(b, k, 2)
                    hot_step(b, k, 3)
                    x1_norm(d, k, 0)

                with dve.Fori(1, T // 2) as i:
                    for k in range(2):
                        both(i * 2 + k, k, i)
                both(T - 1, 0, T // 2)
                for d in range(T - 2, T):
                    x1_sum(d, d % 2, 0)
                    x1_stats(d, d % 2, 0, (d // 2 + 1) * 16)
                    x1_norm(d, d % 2, 0)
            with dve.Else():
                gs = [0]

                def gstep(ins):
                    gs[0] += 1
                    ins.then_inc(g_pro, 1)

                def gsettled():
                    dve.wait_ge(g_pro, gs[0])

                shape = [P, T, NRANGE]

                def over_blocks(r):
                    return r[:, :].rearrange("p (o g) -> p o g", o=1).to_broadcast(shape)

                node_b = block_node[:, :].rearrange("p (t o) -> p t o", o=1).to_broadcast(shape)
                dve.wait_ge(g_dst_in, 16)
                dve.wait_ge(g_consts, 3)
                gstep(v.tensor_reduce(gmin[:, :], dst_gen[:, :].rearrange("p (g c) -> p g c", c=RANGE), AXX, ALU.min))
                gstep(v.tensor_reduce(gmax[:, :], dst_gen[:, :].rearrange("p (g c) -> p g c", c=RANGE), AXX, ALU.max))
                gsettled()
                gstep(v.tensor_tensor(hit[:, :, :], over_blocks(gmax), node_b, ALU.is_ge))
                gstep(v.tensor_tensor(cand[:, :, :], node_b, over_blocks(gmin), ALU.subtract))
                gsettled()
                gstep(v.scalar_tensor_tensor(out=hit[:, :, :], in0=cand[:, :, :], scalar=float(1 - P), in1=hit[:, :, :], op0=ALU.is_ge, op1=ALU.mult))
                gsettled()
                gstep(v.scalar_tensor_tensor(out=cand[:, :, :], in0=over_blocks(gpos), scalar=-BIG, in1=hit[:, :, :], op0=ALU.add, op1=ALU.mult))
                gsettled()
                gstep(v.tensor_reduce(lim[:, 0, :], cand[:, :, :], AXX, ALU.min))
                gsettled()
                gstep(v.scalar_tensor_tensor(out=cand[:, :, :], in0=over_blocks(gpos), scalar=float(RANGE), in1=hit[:, :, :], op0=ALU.add, op1=ALU.mult))
                gsettled()
                gstep(v.tensor_reduce(lim[:, 1, :], cand[:, :, :], AXX, ALU.max))
                assert gs[0] == G_LIM
                dve.wait_ge(lim_turned, 1)
                gstep(v.tensor_reduce(span[:, 0:1], lim_ps[0][0:T, 0:P], AXX, ALU.min))
                gstep(v.tensor_reduce(span[:, 1:2], lim_ps[1][0:T, 0:P], AXX, ALU.max))
                gsettled()
                gstep(v.scalar_tensor_tensor(out=span[:, 0:1], in0=span[:, 0:1], scalar=BIG, in1=span[:, 1:2], op0=ALU.add, op1=ALU.min))
                gsettled()
                gstep(v.tensor_tensor(span[:, 2:3], span[:, 1:2], span[:, 0:1], ALU.subtract))
                gsettled()
                gstep(v.tensor_scalar(over[:, :], batch_starts[:, :], span[:, 2:3], None, ALU.is_lt, ALU.add, accum_out=span[:, 3:4]))
                gsettled()
                gstep(v.tensor_scalar(span[:, 3:4], span[:, 3:4], 1.0, None, ALU.max))
                assert gs[0] == G_SPAN
                dve.wait_ge(table_made, 1)
                for k in range(3):
                    gstep(v.tensor_copy(table[0:1, k, :], table_ps[k]))
                gsettled()
                dve.sem_inc(table_ready, 1)

                with dve.Fori(0, T) as d:
                    _, n, first = block_edges(dve, d)
                    with dve.Fori(0, n) as j:
                        b = first + j
                        dve.wait_ge(dst_in, (b + 1) * 16)
                        dve.wait_ge(onehot_ready, (b + 1) * U)
                        v.tensor_scalar(dst_loc[:, :], dst_ix[:, :], block_node[:, ds(d, 1)], None, ALU.subtract).then_inc(loc_ready, 1)
                        dve.wait_ge(loc_ready, b + 1)
                        dve.sem_inc(dst_free, 1)
                        for u in range(U):
                            dve.wait_ge(slot_free, b * U + (u + 1))
                            v.tensor_scalar(onehot[:, u, :], iota[:, :], dst_loc[:, u:u + 1], None, ALU.is_equal).then_inc(onehot_ready, 1)
                    x1_sum(d, 0, 1)
                    x1_stats(d, 0, 1, d * 16 + 16)
                    x1_norm(d, 0, 1)

            dve.wait_ge(epi, (T + 2) * EPI)
            v.scalar_tensor_tensor(out=shift[:, :], in0=mean[:, :], scalar=-1.0, in1=rstd[:, :], op0=ALU.mult, op1=ALU.mult).then_inc(shift_ready, 1)

            rs = [0]

            def rstep(ins):
                rs[0] += 1
                ins.then_inc(rt, 1)

            def rsettled():
                dve.wait_ge(rt, rs[0])

            def row(i, n=NX):
                return route[0:1, i, 0:n]

            def softmax(out_row, in_row, n, acts):
                rstep(v.tensor_reduce(row(8, 1), in_row, AXX, ALU.max))
                rsettled()
                rstep(v.tensor_scalar(row(9, n), in_row, row(8, 1), None, ALU.subtract))
                dve.wait_ge(rt_act, acts)
                rstep(v.tensor_reduce(row(8, 1), row(10, n), AXX, ALU.add))
                rsettled()
                rstep(v.reciprocal(row(8, 1), row(8, 1)))
                rsettled()
                rstep(v.tensor_scalar(out_row, row(10, n), row(8, 1), None, ALU.mult))
                rsettled()

            dve.wait_ge(zsum_ready, 1)
            rstep(v.tensor_scalar(zmean[:, :], zsum[:, 0:KD], 1.0 / N, None, ALU.mult))
            dve.wait_ge(rt_pe, 1)
            rstep(v.tensor_tensor(row(0), rt_ps[0:1, 0:NX], br[:, :], ALU.add))
            rsettled()
            softmax(row(1), row(0), NX, 1)
            rstep(v.tensor_scalar(row(2), row(1), float(N), None, ALU.mult))
            rsettled()
            rstep(v.reciprocal(row(3), row(2)))
            rsettled()
            rstep(v.tensor_scalar(row(4), row(3), CAP, 1.0, ALU.mult, ALU.min))
            rsettled()
            rstep(v.tensor_tensor(row(5), row(1), row(4), ALU.mult))
            rsettled()
            softmax(row(6), row(5), NX, 2)
            rstep(v.max(row(7), row(6)))
            rsettled()
            rstep(v.max_index(route_ix[:, :], row(7), row(6)))
            assert rs[0] == ROUTE_IX
            softmax(row(11, TOP_K), row(7, TOP_K), TOP_K, 3)
            assert rs[0] == ROUTE_W
            dve.wait_ge(rt_pe, 2)
            rstep(v.tensor_copy(wts[:, :], rt_ps[:, 64:64 + TOP_K]))
            rsettled()
            dve.wait_ge(experts_in, 16 * 4 * TOP_K)
            for k in range(TOP_K):
                w2k = W2e[:, k, :, :].rearrange("p k d -> p (k d)")
                rstep(v.tensor_scalar(w2k, w2k, wts[:, k:k + 1], None, ALU.mult))
            rstep(v.tensor_scalar(b2w[:, :], b2e[:, 0, :], wts[:, 0:1], None, ALU.mult))
            rsettled()
            rstep(v.tensor_copy(W2h[:, :, :, :], W2e[:, :, :, :]))
            rstep(v.scalar_tensor_tensor(out=b2w[:, :], in0=b2e[:, 1, :], scalar=wts[:, 1:2], in1=b2w[:, :],
                                         op0=ALU.mult, op1=ALU.add))
            dve.wait_ge(w1_split, 1)
            rstep(v.tensor_tensor(W1l[:, :, :, :], W1e[:, :, :, :], W1h[:, :, :, :].bitcast(F32), ALU.subtract))
            dve.wait_ge(rt, 28)
            rstep(v.tensor_tensor(W2l[:, :, :, :], W2e[:, :, :, :], W2h[:, :, :, :].bitcast(F32), ALU.subtract))
            assert rs[0] == ROUTE_END and TOP_K == 2

            def split_z(g, k, n):
                for q in range(KD):
                    dve.wait_ge(zh_kept, g * KD + (KD + q + 1))
                    v.tensor_tensor(zTl[:, k, q, 0:n], zt_ps[q][:, 0:n], zTh[:, k, q, 0:n].bitcast(F32), ALU.subtract).then_inc(zl_kept, 1)

            def split_g(g, k, n):
                for c in range(CF):
                    dve.wait_ge(g_made, g * (2 * CF) + (2 * c + 10))
                    v.tensor_tensor(gl[:, k, c, 0:n], gf[:, c % 2, 0:n], gh[:, k, c, 0:n].bitcast(F32), ALU.subtract).then_inc(gl_made, 1)

            def out_stats(g, k, m):
                t = g * GT + m
                e = t * NORM + 2 * NORM
                dve.wait_ge(y_made, t + (2 * GT + 1))
                dve.wait_ge(prep, g * PREP + (2 * PREP + 1))
                dve.wait_ge(done, t * 2 + (2 * GT + 2))
                v.tensor_tensor(pre[:, m, :], y_ps[(k * GT + m) % 2][:, 0:D], zb[:, k, m, :], ALU.add).then_inc(norm, 1)
                hold(dve, norm, e + 1)
                v.bn_stats(stf[:, m, :], pre[:, m, :]).then_inc(norm, 1)
                hold(dve, norm, e + 2)
                v.bn_aggr(mvf[:, m, :], stf[:, m, :]).then_inc(norm, 1)
                dve.wait_ge(norm, e + 3)
                v.tensor_scalar(vare[:, ds(t, 1)], mvf[:, m, 1:2], LN_EPS, None, ALU.add).then_inc(norm, 1)

            def out_end(g, k, m):
                t = g * GT + m
                v.scalar_tensor_tensor(out=pre[:, m, :], in0=pre[:, m, :], scalar=mvf[:, m, 0:1], in1=gamma_bc[:, :],
                                       op0=ALU.subtract, op1=ALU.mult).then_inc(done, 1)
                dve.wait_ge(pow_ready, t + 1)
                dve.wait_ge(done, t * 2 + (4 * GT + 1))
                dve.wait_ge(prep, g * PREP + (2 * PREP + 2))
                dve.wait_ge(res_free, t + 1)
                v.scalar_tensor_tensor(out=res[:, (k * GT + m) % 2, :], in0=pre[:, m, :], scalar=rstdf[:, ds(t, 1)], in1=x1b[:, k, m, :],
                                       op0=ALU.mult, op1=ALU.add).then_inc(done, 1)

            def output(g, k, n):
                out_stats(g, k, 0)
                for m in range(1, n):
                    out_stats(g, k, m)
                    out_end(g, k, m - 1)
                out_end(g, k, n - 1)

            split_z(0, 0, GT * P)
            split_g(0, 0, GT * P)
            split_z(1, 1, GT * P)
            with dve.Fori(0, NG // 2 - 1) as i:
                for k in range(2):
                    split_g(i * 2 + (k + 1), 1 - k, GT * P)
                    split_z(i * 2 + (k + 2), k, GT * P)
                    output(i * 2 + k, k, GT)
            split_g(NG - 1, 1, GT * P)
            split_z(NG, 0, P)
            output(NG - 2, 0, GT)
            split_g(NG, 0, P)
            output(NG - 1, 1, GT)
            output(NG, 0, 1)

        @block.scalar
        def _(act):
            s = nc.scalar
            act.sem_inc(h_kept, 2)
            act.sem_inc(bank_kept, BPS)
            act.sem_inc(low_kept, 2)
            act.sem_inc(zh_kept, KD)
            act.sem_inc(g_made, 8)
            act.wait_ge(consts, N_CONSTS)

            act.wait_ge(dve_pro, STATS)
            s.activation(sd[:, :], mv[:, :, 1], ACT.Sqrt, bias=eps[:, :]).then_inc(sd_made, 1)
            act.wait_ge(dve_pro, RSTD)

            def normalise(t, k):
                act.wait_ge(xn_turned, t + 1)
                s.activation(xn[:, k, :], tile(xs, t), ACT.Identity, scale=rstd[:, ds(t, 1)], bias=shift[:, ds(t, 1)]).then_inc(xn_ready, 1)

            def keep_xnT(t, k):
                act.wait_ge(xn_turned, t + 3)
                s.copy(xnT[:, k, :], turn_ps[k][:, 0:D]).then_inc(xnT_ready, 1)

            def keep_h(t, k):
                act.wait_ge(h_made, t + 1)
                s.copy(tile(hs, t), h_ps[k][:, 0:D]).then_inc(h_kept, 1)

            normalise(0, 0)
            normalise(1, 1)
            keep_xnT(0, 0)
            with act.Fori(0, T // 2 - 1) as i:
                normalise(i * 2 + 2, 0)
                keep_xnT(i * 2 + 1, 1)
                keep_h(i * 2, 0)
                normalise(i * 2 + 3, 1)
                keep_xnT(i * 2 + 2, 0)
                keep_h(i * 2 + 1, 1)
            normalise(T - 1, 0)
            keep_xnT(T - 2, 1)
            keep_h(T - 3, 0)
            keep_xnT(T - 1, 0)
            keep_h(T - 2, 1)
            keep_h(T - 1, 0)

            act.wait_ge(dve_pro, DEG)
            s.activation(sd[:, :], deg_sb[:, :], ACT.Sqrt, bias=ones[:, 0:1]).then_inc(sd_made, 1)
            act.wait_ge(dve_pro, DINV)
            act.wait_ge(h_kept, T + 2)
            act.wait_ge(xn_ready, T)
            with act.Fori(0, T) as t:
                s.activation(tile(tab, t)[:, 0:D], tile(hs, t), ACT.Copy, scale=dinv[:, ds(t, 1)]).then_inc(hi_made, 1)
            act.wait_ge(lo_made, T)

            def keep_low(d, k):
                act.wait_ge(acc_ready, d + 1)
                act.wait_ge(epi, d * EPI + (EPI + 1))
                s.activation(low[:, :], acc[k][:, D:2 * D], ACT.Copy, scale=dinv[:, ds(d, 1)]).then_inc(low_kept, 1)

            def deviation(d):
                act.wait_ge(epi, d * EPI + (2 * EPI + 7))
                s.copy(mean[:, ds(d, 1)], mvb[:, 0:1]).then_inc(sd2_made, 1)
                s.activation(sd[:, 0:1], mvb[:, 1:2], ACT.Sqrt, bias=eps[:, :]).then_inc(sd2_made, 1)

            with act.If(is_dense(act)):
                def keep_counts(b, k, s_):
                    for j in range(BPS):
                        act.wait_ge(bank_ready, b * (STEPS * BPS) + (s_ * BPS + j + 1 + 2 * BPS))
                        at = (s_ * BPS + j) * (2 * KEYS)
                        s.copy(adj[k][:, at:at + 2 * KEYS], adj_ps[j][:, 0:2 * KEYS]).then_inc(bank_kept, 1)

                def counts_and_end(b, k):
                    keep_low(b - 2, k)
                    for s_ in range(STEPS):
                        keep_counts(b, k, s_)
                        if s_ == 2:
                            deviation(b - 2)

                for b in range(2):
                    for s_ in range(STEPS):
                        keep_counts(b, b, s_)
                with act.Fori(1, T // 2) as i:
                    for k in range(2):
                        counts_and_end(i * 2 + k, k)
                counts_and_end(T - 1, 0)
                for d in range(T - 2, T):
                    keep_low(d, d % 2)
                    deviation(d)
            with act.Else():
                with act.Fori(0, T) as d:
                    keep_low(d, 0)
                    deviation(d)

            for i, (at, n) in enumerate(((4, NX), (13, NX), (20, TOP_K))):
                act.wait_ge(rt, at)
                s.activation(route[0:1, 10, 0:n], route[0:1, 9, 0:n], ACT.Exp).then_inc(rt_act, 1)

            def normalise_again(g, k, n, loaded):
                act.wait_ge(x1_in[k], loaded)
                act.wait_ge(z_turned, g + 1)
                act.wait_ge(prep, g * PREP + PREP)
                for m in range(n):
                    t = g * GT + m
                    s.activation(zf[:, k, m, :], x1f[:, k, m, :], ACT.Identity, scale=rstd[:, ds(t, 1)], bias=shift[:, ds(t, 1)]).then_inc(z_made, 1)

            def keep_z(g, k, n):
                act.wait_ge(z_turned, g + 3)
                for q in range(KD):
                    s.copy(zTh[:, k, q, 0:n], zt_ps[q][:, 0:n]).then_inc(zh_kept, 1)

            def gelus(g, k, n, tiles):
                for c in tiles:
                    if c == 0:
                        act.wait_ge(y_made, g * GT + GT)
                    act.wait_ge(h1_made, g * CF + (c + 1))
                    bias = b1e[:, c // KF, c % KF:c % KF + 1]
                    s.activation(gh[:, k, c, 0:n], h1_ps[c % 4][:, 0:n], ACT.Gelu, bias=bias).then_inc(g_made, 1)
                    act.wait_ge(gl_made, g * CF + (c + 1))
                    s.activation(gf[:, c % 2, 0:n], h1_ps[c % 4][:, 0:n], ACT.Gelu, bias=bias).then_inc(g_made, 1)

            act.wait_ge(shift_ready, 1)
            normalise_again(0, 0, GT, 16)
            normalise_again(1, 1, GT, 16)
            keep_z(0, 0, GT * P)
            act.wait_ge(experts_in, 16 * 4 * TOP_K)
            s.copy(W1h[:, :, :, :], W1e[:, :, :, :]).then_inc(w1_split, 1)
            gelus(0, 0, GT * P, range(CF))
            keep_z(1, 1, GT * P)
            half = CF // 2
            with act.Fori(0, NG // 2 - 1) as i:
                for k in range(2):
                    gelus(i * 2 + (k + 1), 1 - k, GT * P, range(half))
                    normalise_again(i * 2 + (k + 2), k, GT, i * 16 + 32)
                    gelus(i * 2 + (k + 1), 1 - k, GT * P, range(half, CF))
                    keep_z(i * 2 + (k + 2), k, GT * P)
            gelus(NG - 1, 1, GT * P, range(half))
            normalise_again(NG, 0, 1, (NG // 2 + 1) * 16)
            gelus(NG - 1, 1, GT * P, range(half, CF))
            keep_z(NG, 0, P)
            gelus(NG, 0, P, range(CF))

        @block.tensor
        def _(pe):
            mm = nc.tensor.matmul
            pe.sem_inc(xn_turned, 2)
            pe.sem_inc(counted, 2)
            pe.sem_inc(bank_ready, 2 * BPS)
            pe.sem_inc(slot_free, U)
            pe.sem_inc(z_turned, 2)
            pe.sem_inc(y_made, 2 * GT)
            pe.wait_ge(consts, N_CONSTS + 1)

            mm(deg[:, 0:T], zero[:, :], zero[:, 0:T], start=True, stop=True)

            def count(c, k):
                pe.wait_ge(ones_ready, c * 2 + 2)
                for q in range(SC):
                    last = mm(deg[:, 0:T], hot_src[:, k, :, q], hot_key[:, k, 0:T, q], start=False, stop=True, skip_group_check=True)
                last.then_inc(counted, 1)

            def turn_x(t, k):
                pe.wait_ge(xn_ready, t + 1)
                for q in range(KD):
                    last = nc.tensor.transpose(turn_ps[k][:, q * P:(q + 1) * P], xn[:, k, q * P:(q + 1) * P], ident[:, :])
                last.then_inc(xn_turned, 1)

            def make_h(t, k):
                pe.wait_ge(xnT_ready, t + 1)
                pe.wait_ge(h_kept, t + 1)
                for q in range(KD):
                    last = mm(h_ps[k][:, 0:D], xnT[:, k, q * P:(q + 1) * P], W[:, q, :], start=(q == 0), stop=(q == KD - 1))
                last.then_inc(h_made, 1)

            with pe.Fori(0, H_FIRST // 2) as i:
                count(i * 2, 0)
                count(i * 2 + 1, 1)
            pe.wait_ge(weights_in, N_WEIGHTS)
            turn_x(0, 0)
            with pe.Fori(0, T // 2) as i:
                for k in range(2):
                    turn_x(i * 2 + (k + 1), 1 - k)
                    count(i * 4 + (H_FIRST + 2 * k), 0)
                    make_h(i * 2 + k, k)
                    count(i * 4 + (H_FIRST + 2 * k + 1), 1)
            make_h(T - 1, 0)
            pe.wait_ge(counted, HSTEPS + 2)
            pe.sem_inc(deg_ready, 1)

            pe.wait_ge(dve_pro, DEG)
            mm(cum_ps[0:T, 0:GROUPS + 1], deg_sb[:, :], below[:, :], start=True, stop=True).then_inc(cum_made, 1)
            pe.wait_ge(dve_pro, CUM)
            mm(flag_ps[0:1, 0:1], unsorted[:, :], ones[:, 0:1], start=True, stop=False)
            mm(flag_ps[0:1, 0:1], crowded[:, :], ones[0:T, 0:1], start=False, stop=True)
            mm(off_ps[0:T, 0:GROUPS + 1], before[:, :], total[:, :], start=True, stop=True).then_inc(off_made, 1)

            def add_loop(d, k):
                pe.wait_ge(low_kept, d + 1)
                pe.wait_ge(epi, d * EPI + 1)
                return mm(acc[k][:, :], ident_r[:, :], tile(tab, d), start=True, stop=True)

            def add_z(d, k):
                pe.wait_ge(epi, d * EPI + 3 * EPI)
                for q in range(KD):
                    last = mm(zsum[:, q:q + 1], zst[:, k, q * P:(q + 1) * P], valid[:, ds(d + 2, 1)], start=False, stop=True, skip_group_check=True)
                last.then_inc(zsum_done, 1)

            pe.wait_ge(zsum_done, 2)
            pe.wait_ge(lo_made, T)
            pe.wait_ge(flag_ready, 1)
            mm(zsum[:, 0:KD], zero[:, :], zero[:, 0:KD], start=True, stop=True)
            with pe.If(is_dense(pe)):
                def count_edges(b, s):
                    pe.wait_ge(hot_ready, b * (2 * STEPS) + (2 * s + 2 + 2 * STEPS))
                    for j in range(BPS):
                        pe.wait_ge(bank_kept, b * (STEPS * BPS) + (s * BPS + j + 1))
                        for h in range(2):
                            for c in range(CPG):
                                q = (j * 2 + h) * CPG + c
                                last = mm(adj_ps[j][:, h * KEYS:(h + 1) * KEYS], hot_src[:, s % 2, :, q], hot_key[:, s % 2, :, q],
                                          start=(c == 0), stop=(c == CPG - 1))
                        last.then_inc(bank_ready, 1)

                def add_rows(k, lo, hi):
                    nodes = adj[k][:, :].rearrange("p (n q) -> p n q", q=T)
                    for q in range(lo, hi):
                        last = mm(acc[k][:, :], nodes[:, :, q], tab[:, q, :], start=False, stop=True, skip_group_check=True)
                    if hi == T:
                        last.then_inc(acc_ready, 1)

                cuts = [T * s // STEPS for s in range(STEPS + 1)]

                def window(d, k, following):
                    for s in range(STEPS):
                        if following:
                            count_edges(d + 1, s)
                        if s == 0:
                            pe.wait_ge(bank_kept, d * (STEPS * BPS) + (STEPS * BPS + BPS))
                            add_loop(d, k)
                        add_rows(k, cuts[s], cuts[s + 1])
                        if s == 1:
                            add_z(d - 2, k)

                for s in range(STEPS):
                    count_edges(0, s)
                with pe.Fori(0, T // 2) as i:
                    for k in range(2):
                        window(i * 2 + k, k, True)
                window(T - 1, 0, False)
                add_z(T - 2, 1)
                add_z(T - 1, 0)
            with pe.Else():
                pe.wait_ge(g_pro, G_LIM)
                for k in range(2):
                    last = nc.tensor.transpose(lim_ps[k][0:T, 0:P], lim[:, k, :], ident[:, :])
                last.then_inc(lim_turned, 1)
                pe.wait_ge(g_pro, G_SPAN)
                for k, (col, mat) in enumerate(((0, ident), (3, ident), (3, before))):
                    last = mm(table_ps[k], span[:, col:col + 1], mat[0:T, 0:T], start=True, stop=True)
                last.then_inc(table_made, 1)

                pe.wait_ge(table_ready, 1)
                pe.sem_inc(zsum_done, 2)
                with pe.Fori(0, T) as d:
                    _, n, first = block_edges(pe, d)
                    pe.wait_ge(low_kept, d + 2)
                    pe.wait_ge(epi, d * EPI + EPI + 1)
                    add_loop(d, 0)
                    with pe.Fori(0, n) as j:
                        b = first + j
                        for u in range(U):
                            pe.wait_ge(onehot_ready, b * U + (u + 1 + U))
                            pe.wait_ge(rows_in[u], (b + 1) * 16)
                            mm(acc[0][:, :], onehot[:, u, :], rows[:, u, :], start=False, stop=True, skip_group_check=True).then_inc(slot_free, 1)
                    pe.wait_ge(slot_free, (first + n + 1) * U)
                    pe.sem_inc(acc_ready, 1)
                    add_z(d, 0)
            pe.wait_ge(zsum_done, T + 4)
            pe.sem_inc(zsum_ready, 1)

            pe.wait_ge(rt, 1)
            for q in range(KD):
                last = mm(rt_ps[0:1, 0:NX], zmean[:, q:q + 1], Wr[:, q, :], start=(q == 0), stop=(q == KD - 1))
            last.then_inc(rt_pe, 1)

            def turn_z(g, k, n):
                pe.wait_ge(z_made, g * GT + n)
                pe.wait_ge(zh_kept, g * KD + KD)
                pe.wait_ge(zl_kept, g * KD + KD)
                for m in range(n):
                    for q in range(KD):
                        last = nc.tensor.transpose(zt_ps[q][:, m * P:(m + 1) * P], zf[:, k, m, q * P:(q + 1) * P], ident[:, :])
                last.then_inc(z_turned, 1)

            def hidden(g, k, n):
                pe.wait_ge(zl_kept, g * KD + 2 * KD)
                for e in range(TOP_K):
                    for f in range(KF):
                        c = e * KF + f
                        pe.wait_ge(g_made, g * (2 * CF) + (2 * c + 2))
                        terms = [(w, z, q) for q in range(KD) for w, z in ((W1h, zTh), (W1h, zTl), (W1l, zTh))]
                        for i, (w, z, q) in enumerate(terms):
                            last = mm(h1_ps[c % 4][:, 0:n], w[:, e, q, f * P:(f + 1) * P], z[:, k, q, 0:n],
                                      start=(i == 0), stop=(i == len(terms) - 1))
                        last.then_inc(h1_made, 1)

            def output(g, k, n):
                pe.wait_ge(gl_made, g * CF + (CF + 2))
                for m in range(n):
                    pe.wait_ge(norm, (g * GT + m) * NORM + 1)
                    terms = [(x_, w, c) for c in range(CF) for x_, w in ((gh, W2h), (gh, W2l), (gl, W2h))]
                    for i, (x_, w, c) in enumerate(terms):
                        last = mm(y_ps[(k * GT + m) % 2][:, 0:D], x_[:, k, c, m * P:(m + 1) * P], w[:, c // KF, c % KF, :],
                                  start=(i == 0), stop=(i == len(terms) - 1))
                    last.then_inc(y_made, 1)

            turn_z(0, 0, GT)
            pe.wait_ge(rt, ROUTE_W)
            mm(rt_ps[:, 64:64 + TOP_K], ones[0:1, :], route[0:1, 11, 0:TOP_K], start=True, stop=True).then_inc(rt_pe, 1)
            pe.wait_ge(rt, ROUTE_END)
            hidden(0, 0, GT * P)
            turn_z(1, 1, GT)
            with pe.Fori(0, NG // 2 - 1) as i:
                for k in range(2):
                    hidden(i * 2 + (k + 1), 1 - k, GT * P)
                    turn_z(i * 2 + (k + 2), k, GT)
                    output(i * 2 + k, k, GT)
            hidden(NG - 1, 1, GT * P)
            turn_z(NG, 0, 1)
            output(NG - 2, 0, GT)
            hidden(NG, 0, P)
            output(NG - 1, 1, GT)
            output(NG, 0, 1)


INPUTS = {"x": "x", "src": "src", "dst": "dst", "L0_gnn_W": "W", "L0_gnn_b": "b", "L0_gnn_prelu_a": "prelu_a",
          "L0_ffn_Wr": "Wr", "L0_ffn_br": "br", "L0_ffn_W1": "W1", "L0_ffn_b1": "b1", "L0_ffn_W2": "W2",
          "L0_ffn_b2": "b2", "L0_ffn_gamma": "gamma", "L0_ffn_beta": "beta"}


def kernel(**inputs):
    import numpy as np
    import concourse.bacc as bacc
    from concourse.bass_utils import run_bass_kernel_spmd

    nc = bacc.Bacc("TRN2", target_bir_lowering=False, num_devices=1)
    n_edges = inputs["src"].shape[0]
    n_nodes = inputs["x"].shape[0]
    n_blocks = -(-n_nodes // P)
    laid_out = {}
    for name, short in INPUTS.items():
        v = np.ascontiguousarray(inputs[name])
        if short in ("src", "dst"):
            nowhere = 0 if short == "src" else n_blocks * P
            v = np.pad(v, (0, padded_edges(n_edges) - n_edges), constant_values=nowhere)
        if short == "x":
            v = np.pad(v, ((0, n_blocks * P - n_nodes), (0, 0)))
        laid_out[short] = v
    laid_out["pairs"] = np.stack([laid_out["src"], laid_out["dst"]], axis=1)
    arrays, args = {}, {}
    for short, v in laid_out.items():
        arrays[f"in_{short}"] = v
        args[short] = nc.dram_tensor(f"in_{short}", v.shape, mybir.dt.from_np(v.dtype), kind="ExternalInput").ap()
    out = nc.dram_tensor("out_0", inputs["x"].shape, F32, kind="ExternalOutput").ap()
    gnn_ffn_kernel(nc, args, out, n_edges)
    r = run_bass_kernel_spmd(nc, [arrays], core_ids=[0])
    return r.results[0]["out_0"]
```

```python
from contextlib import ExitStack

import concourse.bass as bass
from concourse import mybir

ALU = mybir.AluOpType
ACT = mybir.ActivationFunctionType
AXX = mybir.AxisListType.X
F32 = mybir.dt.float32
F32R = mybir.dt.float32r
BF16 = mybir.dt.bfloat16
I32 = mybir.dt.int32
U32 = mybir.dt.uint32
ds = bass.ds

P = 128
LN_EPS = 1e-5
CAPACITY_FACTOR = 1.25
TOP_K = 2

GN = 8
GROUPS = P // GN
CPG = 3
WINDOWS = ((0, 6), (2, 8), (5, 8))
ROWS = GROUPS * CPG
STEPS = 4
SG = GROUPS // STEPS
SC = SG * CPG

SEGS = 2
ROUNDS = 4
RUNS = 8 * ROUNDS

U = 9
PARTS = ((0, 3), (3, 6), (6, 9))
RANGE = 48


def edge_columns(E):
    assert RANGE % (2 * SC) == 0
    return -(-(-(-E // P)) // RANGE) * RANGE


def padded_edges(E):
    return P * edge_columns(E) + max(P * U, edge_columns(E))


def gnn_ffn_kernel(nc, a, out, E):
    x, src, dst, pairs = a["x"], a["src"], a["dst"], a["pairs"]
    N, D = out.shape
    NX, _, F = a["W1"].shape
    T = -(-N // P)
    REST = N - (T - 1) * P
    KD, KF = D // P, F // P
    COLS = edge_columns(E)
    EDGES = P * COLS
    KEYS = GN * T
    SHIFT = 9
    THIRD = (1 << SHIFT) // CPG + 1
    assert all(r // CPG == r * THIRD >> SHIFT for r in range(ROWS))
    MID = KEYS // 2
    WIN = [(lo * T, hi * T) for lo, hi in WINDOWS]
    WIN_AT = [sum(hi - lo for lo, hi in WIN[:j]) * SG for j in range(CPG + 1)]
    HSTEPS = COLS // SC
    SEG = COLS // SEGS
    POS_BITS = SEG.bit_length()
    LOW_BITS = 6
    RSTEPS = -(-SEGS * RUNS // (2 * SC)) * 2
    NRANGE = COLS // RANGE
    BATCH = P * U
    MAXB = -(-EDGES // BATCH) + 1
    BIG = float(EDGES)
    CAP = float(-(-N * CAPACITY_FACTOR // NX))
    GT = 3
    NG = (T - 1) // GT
    LN_TAIL = T // 4 * 4 - 12
    CF = TOP_K * KF
    assert T % 4 == 1 and T == NG * GT + 1 and NG % 2 == 0
    assert T * P << POS_BITS < 1 << 24 and COLS % SEGS == 0 and SEG < 1 << (LOW_BITS + 8)
    assert HSTEPS % 2 == 0 and STEPS % 2 == 0 and KEYS <= 512 and MID <= 256
    assert WIN[0][0] == 0 and WIN[1][1] == WIN[2][1] == KEYS and WIN[1][0] <= WIN[0][1]

    x1_dram = nc.dram_tensor("x1_dram", (T * P, D), F32, kind="Internal").ap()
    starts_dram = nc.dram_tensor("starts_dram", (T, GROUPS), I32, kind="Internal").ap()
    h_table = nc.dram_tensor("h_table", (T * P, 2 * D), F32, kind="Internal").ap()

    with ExitStack() as ctx:
        def sb(name, shape, dt=F32):
            return ctx.enter_context(nc.sbuf_tensor(name, shape, dt))

        def sem(name):
            return ctx.enter_context(nc.semaphore(name))

        x_parts = [(0, 12), (12, 24), (24, 36), (36, T)]

        ident = sb("ident", [P, P])
        ident_r = sb("ident_r", [P, P], F32R)
        iota = sb("iota", [P, P])
        iota_src = sb("iota_src", [P, P, SC], BF16)
        iota_key = sb("iota_key", [P, KEYS, SG], BF16)
        order = sb("order", [ROWS, ROWS], BF16)
        ones = sb("ones", [P, P])
        zero = sb("zero", [P, P])
        dinv = sb("dinv", [P, T])
        eps = sb("eps", [P, 1])
        neg_half = sb("neg_half", [P, 1])
        bias_bc = sb("bias_bc", [P, D])
        slope_bc = sb("slope_bc", [P, D])
        gamma_bc = sb("gamma_bc", [P, D])
        beta_bc = sb("beta_bc", [P, D])
        W = sb("W", [P, KD, D])
        Wr = sb("Wr", [P, KD, NX])
        br = sb("br", [1, NX])
        below = sb("below", [P, 4 * GROUPS + 1])
        before = sb("before", [T, T])
        block_key = sb("block_key", [ROWS, T])
        row_i = sb("row_i", [ROWS, 1], I32)
        row_key = sb("row_key", [ROWS, 1])
        first_key = sb("first_key", [ROWS, T])
        unsorted = sb("unsorted", [P, 1])
        overfull = sb("overfull", [P, SEGS])
        deg_sb = sb("deg_sb", [P, T])
        cum = sb("cum", [T, 4 * GROUPS + 1])
        total = sb("total", [T, GROUPS])
        width = sb("width", [T, 5, GROUPS])
        lost = sb("lost", [T, 4])
        starts = sb("starts", [T, GROUPS], I32)
        runs_flag = sb("runs_flag", [1, 1], I32)
        flag = sb("flag", [1, 1], I32)
        starts_row = sb("starts_row", [1, T * GROUPS], I32)

        hot_src = sb("hot_src", [P, 2, P, SC], BF16)
        hot_key = sb("hot_key", [P, 2, WIN_AT[CPG]], BF16)
        raw = sb("raw", [ROWS, 2, P, 2], I32)
        blk_i = sb("blk_i", [ROWS, P], I32)
        wide = sb("wide", [ROWS, P])
        place_row = sb("place_row", [ROWS, P], BF16)
        key_row = sb("key_row", [ROWS, P], BF16)
        hot_win = [[hot_key[:, k, WIN_AT[j]:WIN_AT[j + 1]].rearrange("p (n c) -> p n c", c=SG) for j in range(CPG)] for k in range(2)]
        hot_blk = [hot_key[:, k, 0:T * SC].rearrange("p (n c) -> p n c", c=SC) for k in range(2)]
        hot_run = [hot_key[:, k, 0:3 * T * SC].rearrange("p (v n c) -> p v n c", v=3, c=SC) for k in range(2)]
        turned = sb("turned", [P, 2, 2, ROWS], BF16)

        xsum = sb("xsum", [P, T])
        neg_mean = sb("neg_mean", [P, T])
        xsq = sb("xsq", [P, T])
        mvb = sb("mvb", [P, 2])
        mean = sb("mean", [P, T])
        sd = sb("sd", [P, T])
        sd1 = sb("sd1", [P, T])
        rstd = sb("rstd", [P, T])
        shift = sb("shift", [P, T])
        stats = sb("stats", [P, 6])
        xin = sb("xin", [P, 2, D])
        x1 = sb("x1", [P, 2, D])
        zst = sb("zst", [P, 2, D])
        low = sb("low", [P, D])
        low_b = sb("low_b", [P, D])
        zacc = sb("zacc", [P, D])
        agg = sb("agg", [P, D])
        neg = sb("neg", [P, D])

        route = sb("route", [1, 12, NX])
        route_ix = sb("route_ix", [1, 8], U32)
        zmean = sb("zmean", [P, KD])
        wts = sb("wts", [P, TOP_K])
        b1e = sb("b1e", [P, TOP_K, KF])

        WORD = 4
        TAB_AT = nc.sbuf_usable_end - (T * 2 * D + 2 * P * T) * WORD
        TAB_AT -= TAB_AT % 64
        ADJ_AT = TAB_AT + T * 2 * D * WORD
        REGION_END = ADJ_AT + 2 * P * T * WORD
        assert nc.sbuf_base <= TAB_AT, (nc.sbuf_base, TAB_AT)

        def tenants(at, end=REGION_END):
            place_at = [at]

            def take(name, shape, dt=F32):
                size = 2 if dt == BF16 else WORD
                for n in shape[1:]:
                    size *= n
                t = nc.alloc_sbuf_tensor_at(name, shape, dt, offset=place_at[0])
                place_at[0] += -(-size // 64) * 64
                assert place_at[0] <= end
                return t
            return take

        tab = tenants(TAB_AT)("tab", [P, T, 2 * D], F32R)
        room = tenants(ADJ_AT)
        adj = [room(f"adj{k}", [P, P * T], F32R) for k in range(2)]
        xs = tenants(ADJ_AT)("xs", [P, T, D])
        room = tenants(TAB_AT, ADJ_AT)
        dst_all = room("dst_all", [P, COLS + 1], I32)
        falls = room("falls", [P, COLS])
        ends = room("ends", [P, COLS])
        position = room("position", [P, COLS])
        mark = [room(f"mark{i}", [P, COLS]) for i in range(2)]
        runs = room("runs", [P, SEGS, RUNS + 1])
        runs_i = room("runs_i", [P, SEGS, RUNS + 1], I32)
        run_pos = room("run_pos", [P, SEGS, RUNS + 1], I32)
        run_int = [room(f"run_int{i}", [P, SEGS, RUNS], I32) for i in range(6)]
        run_val = room("run_val", [P, 4, RSTEPS * SC], BF16)
        low_i = room("low_i", [P, COLS], I32)
        high_i = room("high_i", [P, COLS], I32)
        low7 = room("low7", [P, COLS], BF16)
        high = room("high", [P, COLS], BF16)
        unused_falls = room("unused_falls", [P, COLS], BF16)
        unused = room("unused", [P, T, D], BF16)
        xstats = room("xstats", [P, x_parts[-1][1] - x_parts[-1][0], 6])
        xmv = room("xmv", [P, x_parts[-1][1] - x_parts[-1][0], 2])
        xn = [x1[:, 0, :], x1[:, 1, :], xin[:, 0, :], xin[:, 1, :]]
        xnT = zst
        room = tenants(ADJ_AT)
        rows = room("rows", [P, U, 2 * D])
        onehot = room("onehot", [P, U, P])
        dst_gen = room("dst_gen", [P, COLS], I32)
        hit = room("hit", [P, T, NRANGE])
        cand = room("cand", [P, T, NRANGE])
        gmin, gmax, gpos = (room(n, [P, NRANGE]) for n in ("gmin", "gmax", "gpos"))
        lim = room("lim", [P, 2, T])
        span = room("span", [T, 4])
        batch_starts = room("batch_starts", [T, MAXB])
        over = room("over", [T, MAXB])
        block_node = room("block_node", [P, T])
        table = room("table", [1, 3, T], I32)
        src_ix = [room(f"src_ix{h}", [P, hi - lo], I32) for h, (lo, hi) in enumerate(PARTS)]
        dst_ix = room("dst_ix", [P, U], I32)
        dst_loc = room("dst_loc", [P, U])
        room = tenants(TAB_AT)
        W1e = room("W1e", [P, TOP_K, KD, F])
        W2e = room("W2e", [P, TOP_K, KF, D])
        W1h, W1l = (room(n, [P, TOP_K, KD, F], F32R) for n in ("W1h", "W1l"))
        W2h, W2l = (room(n, [P, TOP_K, KF, D], F32R) for n in ("W2h", "W2l"))
        zTh, zTl = (room(n, [P, 2, KD, GT * P], F32R) for n in ("zTh", "zTl"))
        gh, gl = (room(n, [P, 2, CF, GT * P], F32R) for n in ("gh", "gl"))
        gf = room("gf", [P, 2, GT * P])
        x1f, zf, zb, x1b = (room(n, [P, 2, GT, D]) for n in ("x1f", "zf", "zb", "x1b"))
        pre = room("pre", [P, GT, D])
        res = room("res", [P, 2, D])
        b2e = room("b2e", [P, TOP_K, D])
        b2w = room("b2w", [P, D])
        stf = room("stf", [P, GT, 6])
        mvf = room("mvf", [P, GT, 2])
        vare = room("vare", [P, T])
        rstdf = room("rstdf", [P, T])

        banks = [ctx.enter_context(nc.psum_tensor(f"bank{i}", [P, 512], F32)) for i in range(8)]
        h_ps, turn_ps, deg = banks[0:2], banks[2:4], banks[4]
        cum_ps, off_ps, flag_ps = banks[5], banks[6], banks[7]
        adj_ps, acc, zsum, rt_ps = banks[0:SG], banks[4:6], banks[6], banks[7]
        edge_ps = banks[7][:, 0:2 * ROWS]
        lim_ps = banks[0:2]
        table_ps = [banks[2][0:1, 128 * k:128 * k + T] for k in range(3)]
        zt_ps, h1_ps, y_ps = banks[0:2], banks[2:6], banks[6:8]

        held = sem("held")
        consts = sem("consts")
        position_made = sem("position_made")
        x_in = [sem(f"x_in{i}") for i in range(len(x_parts))]
        edges_in = sem("edges_in")
        weights_in = sem("weights_in")
        dve_pro = sem("dve_pro")
        xstat = sem("xstat")
        sd_made = sem("sd_made")
        xn_ready = sem("xn_ready")
        xn_turned = sem("xn_turned")
        xnT_ready = sem("xnT_ready")
        h_made = sem("h_made")
        ones_ready = sem("ones_ready")
        counted = sem("counted")
        deg_ready = sem("deg_ready")
        unsorted_ready = sem("unsorted_ready")
        runs_checked = sem("runs_checked")
        runs_flag_ready = sem("runs_flag_ready")
        run_hit = sem("run_hit")
        gen_hist = sem("gen_hist")
        cum_made = sem("cum_made")
        off_made = sem("off_made")
        flag_ready = sem("flag_ready")
        starts_out = sem("starts_out")
        starts_in = sem("starts_in")
        hi_made = sem("hi_made")
        lo_made = sem("lo_made")
        raw_in = [sem(f"raw_in{k}") for k in range(2)]
        raw_free = sem("raw_free")
        decoded = sem("decoded")
        edges_turned = sem("edges_turned")
        turned_kept = sem("turned_kept")
        hot_ready = sem("hot_ready")
        bank_ready = sem("bank_ready")
        bank_kept = sem("bank_kept")
        loop_added = sem("loop_added")
        acc_ready = sem("acc_ready")
        low_kept = sem("low_kept")
        low_biased = sem("low_biased")
        epi = sem("epi")
        sd2_made = sem("sd2_made")
        tile_in = [sem(f"tile_in{k}") for k in range(2)]
        x1_stored = [sem(f"x1_stored{k}") for k in range(2)]
        x1_out = sem("x1_out")
        zacc_clear = sem("zacc_clear")
        zsum_done = sem("zsum_done")
        g_dst_in = sem("g_dst_in")
        g_consts = sem("g_consts")
        g_pro = sem("g_pro")
        h_stored = sem("h_stored")
        lim_turned = sem("lim_turned")
        table_made = sem("table_made")
        table_ready = sem("table_ready")
        src_in = [sem(f"src_in{h}") for h in range(len(PARTS))]
        dst_in = sem("dst_in")
        dst_free = sem("dst_free")
        rows_in = [sem(f"rows_in{u}") for u in range(U)]
        loc_ready = sem("loc_ready")
        onehot_ready = sem("onehot_ready")
        slot_free = sem("slot_free")
        zsum_ready = sem("zsum_ready")
        rt = sem("rt")
        rt_pe = sem("rt_pe")
        rt_act = sem("rt_act")
        w1_in = sem("w1_in")
        w2_in = sem("w2_in")
        w_split = sem("w_split")
        x1_in = [sem(f"x1_in{k}") for k in range(2)]
        shift_ready = sem("shift_ready")
        z_made = sem("z_made")
        prep = sem("prep")
        z_turned = sem("z_turned")
        zh_kept = sem("zh_kept")
        zl_kept = sem("zl_kept")
        h1_made = sem("h1_made")
        g_made = sem("g_made")
        gl_made = sem("gl_made")
        y_made = sem("y_made")
        norm = sem("norm")
        pow_ready = sem("pow_ready")
        done = sem("done")
        res_stored = sem("res_stored")
        res_free = sem("res_free")

        N_CONSTS = 19 + CPG
        N_WEIGHTS = 16 * 7
        EPI = 8
        NORM = 4
        PREP = 2
        ROUTE_IX, ROUTE_W, ROUTE_WTS, ROUTE_W1, ROUTE_END = 18, 23, 24, 26, 29

        FALLS, MARKS = 4, 8
        FOUND = MARKS + SEGS * (2 * ROUNDS - 1) + 2
        XSTAT = FOUND + 12 + 2 * (x_parts[-1][1] - x_parts[-1][0]) + 2
        DEG = XSTAT + 2
        DINV = DEG + 1
        RSTD = DINV + 1
        CUM = RSTD + 11
        STARTS = CUM + 1
        G_LIM, G_SPAN = 9, 15

        block = ctx.enter_context(nc.Block())

        def hold(eng, semaphore, value):
            eng.wait_ge(semaphore, value)
            eng.sem_inc(held, 1)

        def tile(buf, t):
            return buf[:, ds(t, 1), :].rearrange("p o d -> p (o d)")

        def is_dense(eng):
            eng.wait_ge(flag_ready, 1)
            return eng.value_load(flag[0:1, 0:1], min_val=0, max_val=EDGES + 4 * T * GROUPS) == 0

        def by_runs(eng):
            eng.wait_ge(runs_flag_ready, 1)
            return eng.value_load(runs_flag[0:1, 0:1], min_val=0, max_val=EDGES + P * SEGS) == 0

        def block_edges(eng, d):
            return (eng.value_load(table[0:1, 0, ds(d, 1)], min_val=0, max_val=EDGES),
                    eng.value_load(table[0:1, 1, ds(d, 1)], min_val=1, max_val=MAXB),
                    eng.value_load(table[0:1, 2, ds(d, 1)], min_val=0, max_val=MAXB * T))

        def x1_group(g, n):
            return x1_dram[ds(g * (GT * P), n * P), :].rearrange("(t p) d -> p t d", p=P)

        @block.sync
        def _(sp):
            sp.sem_inc(res_free, 2)
            sp.dma_start(dst_all[:, 0:COLS], dst[0:EDGES].rearrange("(p c) -> p c", p=P)).then_inc(edges_in, 16)
            with nc.allow_non_contiguous_dma(reason="the edge after each partition's last, once"):
                sp.dma_start(dst_all[:, COLS:COLS + 1], dst[COLS:COLS + EDGES].rearrange("(p c) -> p c", p=P)[:, 0:1]).then_inc(edges_in, 16)
            for i, (lo, hi) in enumerate(x_parts):
                sp.dma_start(xs[:, lo:hi, :], x[lo * P:hi * P, :].rearrange("(t p) d -> p t d", p=P)).then_inc(x_in[i], 16)
            sp.dma_start(W[:, :, :], a["W"].rearrange("(k p) n -> p k n", p=P)).then_inc(weights_in, 16)
            sp.dma_start(Wr[:, :, :], a["Wr"].rearrange("(k p) n -> p k n", p=P)).then_inc(weights_in, 16)
            sp.dma_start(br[:, :], a["br"].rearrange("(o n) -> o n", o=1)).then_inc(weights_in, 16)
            for buf, name in ((bias_bc, "b"), (slope_bc, "prelu_a"), (gamma_bc, "gamma"), (beta_bc, "beta")):
                sp.dma_start(buf[:, :], a[name].rearrange("(o n) -> o n", o=1).to_broadcast([P, D])).then_inc(weights_in, 16)

            sp.wait_ge(dve_pro, STARTS)
            sp.dma_start(starts_dram[:, :], starts[:, :]).then_inc(starts_out, 16)
            sp.wait_ge(starts_out, 16)
            sp.dma_start(starts_row[:, :], starts_dram.rearrange("(o t) g -> o (t g)", o=1)).then_inc(starts_in, 16)

            sp.wait_ge(starts_in, 16)
            with sp.If(is_dense(sp)):
                def load_edges(d, k):
                    hold(sp, raw_free, d + 1)
                    for g in range(GROUPS):
                        e = nc.s_assert_within(sp.value_load(starts_row[0:1, ds(d * GROUPS + g, 1)]), 0, EDGES,
                                               skip_runtime_bounds_check_because="counts of edges sum to at most all of them")
                        sp.dma_start(raw[g * CPG:(g + 1) * CPG, k, :, :].rearrange("j p s -> j (p s)"),
                                     pairs[ds(e, P * CPG), :].rearrange("(j p) s -> j (p s)", j=CPG)).then_inc(raw_in[k], 16)

                with sp.Fori(0, T // 2) as i:
                    load_edges(i * 2, 0)
                    load_edges(i * 2 + 1, 1)
                load_edges(T - 1, 0)
            with sp.Else():
                sp.wait_ge(lo_made, T + 2)
                sp.dma_start(dst_gen[:, :], dst[0:EDGES].rearrange("(p c) -> p c", p=P)).then_inc(g_dst_in, 16)
                sp.dma_start(h_table.rearrange("(t p) d -> p t d", p=P), tab[:, :, :].bitcast(F32)).then_inc(h_stored, 16)
                sp.wait_ge(table_ready, 1)
                with sp.Fori(0, T) as d:
                    start, n, first = block_edges(sp, d)
                    with sp.Fori(0, n) as j:
                        b = first + j
                        at = nc.s_assert_within(start + j * BATCH, 0, EDGES, skip_runtime_bounds_check_because="a block's last batch starts before its last edge")

                        def edges(t, lo, hi):
                            return t[ds(at, BATCH)].rearrange("(p u) -> p u", u=U)[:, lo:hi]

                        for h, (lo, hi) in enumerate(PARTS):
                            sp.wait_ge(slot_free, b * U + hi)
                            sp.dma_start(src_ix[h][:, :], edges(src, lo, hi)).then_inc(src_in[h], 16)
                            if h == 0:
                                sp.wait_ge(dst_free, b + 1)
                                sp.dma_start(dst_ix[:, :], edges(dst, 0, U)).then_inc(dst_in, 16)

            sp.wait_ge(x1_out, T + 2)
            sp.wait_ge(rt, ROUTE_IX)
            chosen = [sp.value_load(route_ix[0:1, k:k + 1], min_val=0, max_val=NX - 1) for k in range(TOP_K)]
            for k, e in enumerate(chosen):
                sp.dma_start(W1e[:, k, :, :], a["W1"][ds(e, 1), :, :].rearrange("e (k p) f -> p (e k) f", p=P)).then_inc(w1_in, 16)
                with nc.allow_non_contiguous_dma(reason="512 biases, once"):
                    sp.dma_start(b1e[:, k, :], a["b1"][ds(e, 1), :].rearrange("e (k p) -> p (e k)", p=P)).then_inc(w1_in, 16)
            for k, e in enumerate(chosen):
                sp.dma_start(W2e[:, k, :, :], a["W2"][ds(e, 1), :, :].rearrange("e (k p) d -> p (e k) d", p=P)).then_inc(w2_in, 16)
                sp.dma_start(b2e[:, k, :], a["b2"][ds(e, 1), :].to_broadcast([P, D])).then_inc(w2_in, 16)

            def store(t, kk, n):
                sp.wait_ge(done, t * 2 + (2 * GT * 2 + 2))
                sp.dma_start(out[ds(t * P, n), :], res[0:n, kk, :]).then_inc(res_stored, 16)
                sp.wait_ge(res_stored, t * 16 + 16)
                sp.sem_inc(res_free, 1)

            with sp.Fori(0, T // 2) as i:
                for k in range(2):
                    store(i * 2 + k, k, P)
            store(T - 1, 0, REST)

        @block.gpsimd
        def _(pool):
            g = nc.gpsimd
            pool.sem_inc(x1_out, 2)
            g.iota(position[:, :], [[0, SEGS], [1, SEG]], base=1, channel_multiplier=0, allow_small_or_imprecise_dtypes=True).then_inc(position_made, 1)
            for buf, pattern, base, m in ((iota[:, :], [[1, P]], 0, 0),
                                          (iota_src[:, :, :], [[1, P], [0, SC]], 0, 0),
                                          (iota_key[:, :, :], [[1, KEYS], [0, SG]], -MID, 0),
                                          (block_key[:, :], [[-P * T, T]], 0, 0),
                                          (row_i[:, :], [[0, 1]], 0, THIRD)):
                g.iota(buf, pattern, base=base, channel_multiplier=m, allow_small_or_imprecise_dtypes=True).then_inc(consts, 1)
            for buf, value in ((ident, 0.0), (order, 0.0), (ones, 1.0), (zero, 0.0), (before, 1.0), (below, 1.0), (eps, LN_EPS), (neg_half, -0.5)):
                g.memset(buf[:, :], value).then_inc(consts, 1)
            pool.wait_ge(consts, N_CONSTS - 6 - CPG)
            g.affine_select(out=ident[:, :], in_=ident[:, :], compare_op=ALU.not_equal, fill=1.0, base=0,
                            pattern=[[-1, P]], channel_multiplier=1).then_inc(consts, 1)
            g.affine_select(out=before[:, :], in_=before[:, :], compare_op=ALU.is_gt, fill=0.0, base=0,
                            pattern=[[1, T]], channel_multiplier=-1).then_inc(consts, 1)
            for j in range(CPG):
                cols = order[:, j * GROUPS:(j + 1) * GROUPS]
                g.affine_select(out=cols, in_=cols, compare_op=ALU.not_equal, fill=1.0, base=-j,
                                pattern=[[-CPG, GROUPS]], channel_multiplier=1).then_inc(consts, 1)
            for i, (n, node) in enumerate(((GROUPS + 1, 0), (GROUPS, WINDOWS[2][0]), (GROUPS, WINDOWS[0][1]), (GROUPS, WINDOWS[1][0]))):
                cols = below[:, i * GROUPS + min(i, 1):i * GROUPS + min(i, 1) + n]
                g.affine_select(out=cols, in_=cols, compare_op=ALU.is_gt, fill=0.0, base=node,
                                pattern=[[GN, n]], channel_multiplier=-1).then_inc(consts, 1)
            def load_tile(d, k):
                g.dma_start(xin[:, k, :], x[ds(d * P, P), :]).then_inc(tile_in[k], 16)

            pool.sem_inc(low_biased, 1)
            pool.sem_inc(zsum_done, 2)
            g.memset(zacc[:, :], 0.0).then_inc(zacc_clear, 1)
            pool.wait_ge(zacc_clear, 1)

            def add_bias(d):
                hold(pool, low_kept, d + 3)
                pool.wait_ge(epi, d * EPI + (EPI + 1))
                g.tensor_tensor(low_b[:, :], low[:, :], bias_bc[:, :], ALU.add).then_inc(low_biased, 1)

            def store_x1(d, k):
                hold(pool, epi, d * EPI + (2 * EPI + 4))
                g.dma_start(x1_dram[ds(d * P, P), :], x1[:, k, :]).then_inc(x1_stored[k], 16)

            def finish_x1(k, stored):
                hold(pool, x1_stored[k], stored)
                pool.sem_inc(x1_out, 1)

            def add_z(d, k, n):
                hold(pool, zsum_done, d + 2)
                pool.wait_ge(epi, d * EPI + 3 * EPI)
                g.tensor_tensor(zacc[0:n, :], zacc[0:n, :], zst[0:n, k, :], ALU.add).then_inc(zsum_done, 1)

            with pool.If(is_dense(pool)):
                def add_loop(d, k):
                    hold(pool, bank_kept, d * (STEPS * SG) + (STEPS * SG + SG))
                    own = adj[k][:, :].rearrange("p (n q) -> p n q", q=T)[:, :, ds(d, 1)].rearrange("p n o -> p (n o)")
                    g.tensor_tensor(own, own.bitcast(F32), ident[:, :], ALU.add).then_inc(loop_added, 1)

                def ends(d, k, turn, ahead=True):
                    add_bias(d)
                    add_z(d - 1, 1 - k, P)
                    if ahead:
                        add_loop(d + 2, k)
                    store_x1(d, k)
                    if ahead:
                        load_tile(d + 2, k)
                    finish_x1(k, turn * 16 + 16)

                pool.wait_ge(lo_made, T + 2)
                load_tile(0, 0)
                load_tile(1, 1)
                add_loop(0, 0)
                add_loop(1, 1)
                add_bias(0)
                add_loop(2, 0)
                store_x1(0, 0)
                load_tile(2, 0)
                finish_x1(0, 16)
                with pool.Fori(0, T // 2 - 1) as i:
                    ends(i * 2 + 1, 1, i)
                    ends(i * 2 + 2, 0, i + 1)
                ends(T - 2, 1, T // 2 - 1, False)
                ends(T - 1, 0, T // 2, False)
                add_z(T - 1, 0, REST)
            with pool.Else():
                pool.wait_ge(lo_made, T + 2)
                for buf, pattern, m in ((gpos, [[RANGE, NRANGE]], COLS), (block_node, [[P, T]], 0), (batch_starts, [[BATCH, MAXB]], 0)):
                    g.iota(buf[:, :], pattern, base=0, channel_multiplier=m, allow_small_or_imprecise_dtypes=True).then_inc(g_consts, 1)
                pool.wait_ge(table_ready, 1)
                pool.wait_ge(h_stored, 16)
                def gathers(d, nodes):
                    load_tile(d, 0)
                    _, n, first = block_edges(pool, d)
                    with pool.Fori(0, n) as j:
                        b = first + j
                        for h, (lo, hi) in enumerate(PARTS):
                            pool.wait_ge(src_in[h], (b + 1) * 16)
                            for u in range(lo, hi):
                                hold(pool, slot_free, b * U + (u + 1))
                                g.indirect_dma_start(
                                    out=rows[:, u, :], out_offset=None, in_=h_table,
                                    in_offset=bass.IndirectOffsetOnAxis(ap=src_ix[h][:, u - lo:u - lo + 1], axis=0),
                                    bounds_check=T * P - 1).then_inc(rows_in[u], 16)
                    add_bias(d)
                    store_x1(d, 0)
                    finish_x1(0, d * 16 + 16)
                    add_z(d, 0, nodes)

                with pool.Fori(0, T - 1) as d:
                    gathers(d, P)
                gathers(T - 1, REST)

            pool.sem_inc(prep, 2 * PREP)

            def bc(row, n):
                return row[:, :].rearrange("p (o d) -> p o d", o=1).to_broadcast([P, n, D])

            def prepare(gr, k, n, ahead):
                hold(pool, done, gr * (2 * GT) + 2 * GT)
                hold(pool, z_made, gr * GT + n)
                g.tensor_tensor(zb[:, k, 0:n, :], zf[:, k, 0:n, :], bc(b2w, n), ALU.add).then_inc(prep, 1)
                g.tensor_tensor(x1b[:, k, 0:n, :], x1f[:, k, 0:n, :], bc(beta_bc, n), ALU.add).then_inc(prep, 1)
                if ahead:
                    hold(pool, prep, gr * PREP + 3 * PREP)
                    g.dma_start(x1f[:, k, 0:ahead, :], x1_group(gr + 2, ahead)).then_inc(x1_in[k], 16)

            def power(t):
                hold(pool, norm, t * NORM + 3 * NORM)
                g.tensor_tensor(rstdf[:, ds(t, 1)], vare[:, ds(t, 1)], neg_half[:, :], ALU.pow).then_inc(pow_ready, 1)

            pool.wait_ge(x1_out, T + 2)
            for k in range(2):
                g.dma_start(x1f[:, k, :, :], x1_group(k, GT)).then_inc(x1_in[k], 16)
            pool.wait_ge(rt, ROUTE_END)
            prepare(0, 0, GT, GT)
            prepare(1, 1, GT, GT)
            def powers_and_next(gr, k, n, ahead):
                for m in range(GT):
                    power(gr * GT + m)
                prepare(gr + 2, k, n, ahead)

            with pool.Fori(0, NG // 2 - 2) as i:
                for k in range(2):
                    powers_and_next(i * 2 + k, k, GT, GT)
            powers_and_next(NG - 4, 0, GT, 1)
            powers_and_next(NG - 3, 1, GT, 0)
            powers_and_next(NG - 2, 0, 1, 0)
            for t in range((NG - 1) * GT, T):
                power(t)

        @block.vector
        def _(dve):
            v = nc.vector
            pro = [0]

            def step(ins):
                pro[0] += 1
                ins.then_inc(dve_pro, 1)

            def settled():
                dve.wait_ge(dve_pro, pro[0])

            dve.sem_inc(raw_free, 2)
            dve.sem_inc(epi, 2 * EPI)
            dve.sem_inc(dst_free, 1)
            dve.sem_inc(onehot_ready, U)
            dve.sem_inc(zl_kept, KD)
            dve.sem_inc(gl_made, 2)
            dve.sem_inc(norm, 2 * NORM)
            dve.sem_inc(done, 4 * GT)

            dve.wait_ge(edges_in, 32)
            step(v.memset(runs[:, :, :], 0.0))
            step(v.memset(run_val[:, :, :], 0.0))
            step(v.tensor_tensor(ends[:, :], dst_all[:, 0:COLS], dst_all[:, 1:COLS + 1], ALU.is_lt))
            step(v.tensor_tensor(falls[:, :], dst_all[:, 0:COLS], dst_all[:, 1:COLS + 1], ALU.is_gt))
            settled()
            step(v.memset(ends[:, :].rearrange("p (s c) -> p s c", s=SEGS)[:, :, SEG - 1:SEG], 1.0))
            dve.wait_ge(position_made, 1)
            step(v.scalar_tensor_tensor(out=mark[1][:, :], in0=dst_all[:, 0:COLS], scalar=float(1 << POS_BITS), in1=position[:, :],
                                        op0=ALU.mult, op1=ALU.add))
            settled()
            step(v.tensor_tensor(mark[0][:, :], mark[1][:, :], ends[:, :], ALU.mult))
            dve.wait_ge(consts, N_CONSTS)
            step(v.tensor_scalar(row_i[:, :], row_i[:, :], SHIFT, None, ALU.logical_shift_right))
            assert pro[0] == MARKS
            settled()
            for r in range(ROUNDS):
                for i in range(SEGS):
                    seg = slice(i * SEG, (i + 1) * SEG)
                    step(v.max(runs[:, i, r * 8:(r + 1) * 8], mark[r % 2][:, seg]))
                settled()
                if r < ROUNDS - 1:
                    for i in range(SEGS):
                        seg = slice(i * SEG, (i + 1) * SEG)
                        step(v.match_replace(mark[1 - r % 2][:, seg], runs[:, i, r * 8:(r + 1) * 8], mark[r % 2][:, seg], 0.0))
                    settled()
            step(v.tensor_scalar(overfull[:, :], runs[:, :, RUNS - 1], 0.0, None, ALU.is_gt))
            step(v.tensor_copy(runs_i[:, :, :], runs[:, :, :]))
            assert pro[0] == FOUND
            settled()
            node, count, low_n, high_n, low_c, high_c = (t[:, :, :] for t in run_int)
            step(v.tensor_scalar(node, runs_i[:, :, 0:RUNS], POS_BITS, None, ALU.logical_shift_right))
            step(v.tensor_scalar(run_pos[:, :, :], runs_i[:, :, :], (1 << POS_BITS) - 1, None, ALU.bitwise_and))
            settled()
            step(v.tensor_tensor(count, run_pos[:, :, 0:RUNS], run_pos[:, :, 1:RUNS + 1], ALU.subtract))
            step(v.tensor_scalar(low_n, node, P - 1, None, ALU.bitwise_and))
            step(v.tensor_scalar(high_n, node, P.bit_length() - 1, None, ALU.logical_shift_right))
            settled()
            step(v.tensor_scalar(low_c, count, (1 << LOW_BITS) - 1, None, ALU.bitwise_and))
            step(v.tensor_scalar(row_key[:, :], row_i[:, :], float(-KEYS), float(-MID), ALU.mult, ALU.add))
            settled()
            step(v.tensor_tensor(high_c, count, low_c, ALU.subtract))
            settled()
            for i, val in enumerate((low_n, high_n, low_c, high_c)):
                step(v.tensor_copy(run_val[:, i, 0:SEGS * RUNS].rearrange("p (s r) -> p s r", s=SEGS), val))
            settled()
            v.tensor_copy(ident_r[:, :], ident[:, :]).then_inc(consts, 1)
            v.tensor_scalar(first_key[:, :], block_key[:, :], row_key[:, :], None, ALU.add).then_inc(decoded, 1)

            dve.wait_ge(runs_checked, 1)
            v.tensor_copy(runs_flag[:, :], flag_ps[0:1, 8:9]).then_inc(runs_flag_ready, 1)

            def one_hot(hot, numbers, values):
                n, c = hot.shape[1], hot.shape[2]
                return v.tensor_tensor(hot, numbers, values.rearrange("p (o c) -> p o c", o=1).to_broadcast([P, n, c]), ALU.is_equal)

            with dve.If(by_runs(dve)):
                def run_step(c, k):
                    cols = ds(c * SC, SC)
                    dve.wait_ge(counted, c + 1)
                    one_hot(hot_run[k][:, 2], iota_src[:, 0:T, :], run_val[:, 1, cols]).then_inc(run_hit, 1)
                    one_hot(hot_src[:, k, :, :], iota_src[:, :, :], run_val[:, 0, cols]).then_inc(ones_ready, 1)
                    dve.wait_ge(run_hit, c + 1)
                    for i in range(2):
                        v.tensor_tensor(hot_run[k][:, i], hot_run[k][:, 2],
                                        run_val[:, 2 + i, cols].rearrange("p (o c) -> p o c", o=1).to_broadcast([P, T, SC]), ALU.mult).then_inc(ones_ready, 1)

                with dve.Fori(0, RSTEPS // 2) as i:
                    run_step(i * 2, 0)
                    run_step(i * 2 + 1, 1)
            with dve.Else():
                def degree_step(c, k):
                    dve.wait_ge(counted, c + 1)
                    one_hot(hot_src[:, k, :, :], iota_src[:, :, :], low7[:, ds(c * SC, SC)]).then_inc(ones_ready, 1)
                    one_hot(hot_blk[k], iota_src[:, 0:T, :], high[:, ds(c * SC, SC)]).then_inc(ones_ready, 1)

                v.tensor_scalar(low_i[:, :], dst_all[:, 0:COLS], P - 1, None, ALU.bitwise_and).then_inc(gen_hist, 1)
                v.tensor_scalar(high_i[:, :], dst_all[:, 0:COLS], P.bit_length() - 1, None, ALU.logical_shift_right).then_inc(gen_hist, 1)
                dve.wait_ge(gen_hist, 2)
                v.tensor_copy(low7[:, :], low_i[:, :]).then_inc(gen_hist, 1)
                v.tensor_copy(high[:, :], high_i[:, :]).then_inc(gen_hist, 1)
                dve.wait_ge(gen_hist, 4)
                with dve.Fori(0, HSTEPS // 2) as i:
                    degree_step(i * 2, 0)
                    degree_step(i * 2 + 1, 1)

            lo, hi = x_parts[-1]
            dve.wait_ge(x_in[-1], 16)
            for t in range(lo, hi):
                step(v.bn_stats(xstats[:, t - lo, :], xs[:, t, :]))
            settled()
            for t in range(lo, hi):
                step(v.bn_aggr(xmv[:, t - lo, :], xstats[:, t - lo, :]))
            settled()
            step(v.tensor_scalar(neg_mean[:, lo:hi], xmv[:, :, 0], -1.0, None, ALU.mult))
            step(v.tensor_scalar(xsq[:, lo:hi], xmv[:, :, 1], float(D), None, ALU.mult))
            assert pro[0] == XSTAT
            dve.wait_ge(deg_ready, 1)
            step(v.tensor_copy(deg_sb[:, :], deg[:, 0:T]))
            settled()
            step(v.tensor_tensor(deg_sb[:, :], deg_sb[:, :], deg[:, T:2 * T], ALU.add))
            assert pro[0] == DEG
            dve.wait_ge(sd_made, 1)
            step(v.reciprocal(dinv[:, :], sd[:, :]))
            assert pro[0] == DINV
            dve.wait_ge(sd_made, 2)
            step(v.reciprocal(rstd[:, :], sd1[:, :]))
            assert pro[0] == RSTD
            settled()

            def normalise(t, k):
                dve.wait_ge(xn_turned, t + 1)
                v.tensor_scalar(xn[k], tile(xs, t), neg_mean[:, ds(t, 1)], rstd[:, ds(t, 1)], ALU.add, ALU.mult).then_inc(xn_ready, 1)

            for t in range(4):
                normalise(t, t)
            dve.wait_ge(cum_made, 1)
            step(v.tensor_copy(cum[:, :], cum_ps[0:T, 0:4 * GROUPS + 1]))
            settled()
            step(v.tensor_copy(total[:, :], cum[:, GROUPS:GROUPS + 1].to_broadcast([T, GROUPS])))
            for i, at in enumerate((1, GROUPS + 1, 2 * GROUPS + 1, 3 * GROUPS + 1)):
                step(v.tensor_tensor(width[:, i, :], cum[:, at:at + GROUPS], cum[:, 0:GROUPS], ALU.subtract))
            settled()
            step(v.scalar_tensor_tensor(out=width[:, 4, :], in0=width[:, 0, :], scalar=float(P), in1=width[:, 2, :], op0=ALU.min, op1=ALU.subtract))
            settled()
            for i, (w, most) in enumerate(((0, CPG * P), (1, 2 * P), (3, P), (4, 0))):
                step(v.tensor_scalar(width[:, w, :], width[:, w, :], float(most), None, ALU.is_gt, ALU.add, accum_out=lost[:, i:i + 1]))
            assert pro[0] == CUM
            dve.wait_ge(off_made, 1)
            step(v.tensor_tensor(starts[:, :], cum[:, 0:GROUPS], off_ps[0:T, 0:GROUPS], ALU.add))
            assert pro[0] == STARTS
            v.tensor_copy(flag[:, :], flag_ps[0:1, 0:1]).then_inc(flag_ready, 1)
            dve.sem_inc(lo_made, 2)

            def low_part(t, k):
                dve.wait_ge(hi_made, t + 1)
                v.scalar_tensor_tensor(out=tile(tab, t)[:, D:2 * D], in0=h_ps[k][:, 0:D], scalar=dinv[:, ds(t, 1)],
                                       in1=tile(tab, t)[:, 0:D].bitcast(F32), op0=ALU.mult, op1=ALU.subtract).then_inc(lo_made, 1)

            with dve.Fori(0, LN_TAIL // 4) as i:
                for m in range(4):
                    normalise(i * 4 + (m + 4), m)
                    low_part(i * 4 + m, m % 2)

            def last_tiles(between):
                for t in range(LN_TAIL, T):
                    if t + 4 < T:
                        normalise(t + 4, t % 4)
                    low_part(t, t % 2)
                    if t in between:
                        between[t]()
                dve.wait_ge(lo_made, T + 2)
                dve.wait_ge(weights_in, N_WEIGHTS)

            def x1_sum(d, k, alone):
                e = d * EPI + 2 * EPI
                dve.wait_ge(epi, e)
                dve.wait_ge(acc_ready, d + 1)
                dve.wait_ge(low_biased, d + 2)
                v.scalar_tensor_tensor(out=agg[:, :], in0=acc[k][:, 0:D], scalar=dinv[:, ds(d, 1)], in1=low_b[:, :],
                                       op0=ALU.mult, op1=ALU.add).then_inc(epi, 1)
                dve.wait_ge(epi, e + 1)
                v.scalar_tensor_tensor(out=neg[:, :], in0=agg[:, :], scalar=0.0, in1=slope_bc[:, :], op0=ALU.min, op1=ALU.mult).then_inc(epi, 1)
                dve.wait_ge(epi, e + 2)
                v.scalar_tensor_tensor(out=agg[:, :], in0=agg[:, :], scalar=0.0, in1=neg[:, :], op0=ALU.max, op1=ALU.add).then_inc(epi, 1)

            def x1_stats(d, k, alone, loaded):
                e = d * EPI + 2 * EPI
                dve.wait_ge(epi, e + 3)
                dve.wait_ge(tile_in[k], loaded)
                dve.wait_ge(x1_out, d + (1 + alone))
                v.tensor_tensor(x1[:, k, :], xin[:, k, :], agg[:, :], ALU.add).then_inc(epi, 1)
                hold(dve, epi, e + 4)
                v.bn_stats(stats[:, :], x1[:, k, :]).then_inc(epi, 1)
                hold(dve, epi, e + 5)
                v.bn_aggr(mvb[:, :], stats[:, :]).then_inc(epi, 1)

            def x1_norm(d, k, alone):
                e = d * EPI + 2 * EPI
                hold(dve, sd2_made, d * 2 + 2)
                v.reciprocal(rstd[:, ds(d, 1)], sd[:, 0:1]).then_inc(epi, 1)
                dve.wait_ge(epi, e + 7)
                dve.wait_ge(zsum_done, d + (1 + alone))
                v.tensor_scalar(zst[:, k, :], x1[:, k, :], mvb[:, 0:1], rstd[:, ds(d, 1)], ALU.subtract, ALU.mult).then_inc(epi, 1)

            with dve.If(is_dense(dve)):
                def decode(b, k, loaded):
                    source, target = raw[:, k, :, 0], raw[:, k, :, 1]
                    dve.wait_ge(raw_in[k], loaded)
                    v.tensor_scalar(blk_i[:, :], source, P.bit_length() - 1, None, ALU.logical_shift_right).then_inc(decoded, 1)
                    dve.wait_ge(decoded, b * 4 + 2)
                    dve.wait_ge(edges_turned, b + 1)
                    v.scalar_tensor_tensor(out=place_row[:, :], in0=blk_i[:, :], scalar=float(-P), in1=source, op0=ALU.mult, op1=ALU.add).then_inc(decoded, 1)
                    v.scalar_tensor_tensor(out=wide[:, :], in0=target, scalar=float(T), in1=blk_i[:, :], op0=ALU.mult, op1=ALU.add).then_inc(decoded, 1)
                    dve.wait_ge(decoded, b * 4 + 4)
                    dve.sem_inc(raw_free, 1)
                    v.tensor_scalar(key_row[:, :], wide[:, :], first_key[:, ds(b, 1)], float(MID), ALU.add, ALU.min).then_inc(decoded, 1)

                def source_rows(b, k, s):
                    kk = s % 2
                    if s == 0:
                        dve.wait_ge(turned_kept, b + 1)
                    dve.wait_ge(bank_ready, b * (STEPS * SG) + (s + 1) * SG)
                    v.tensor_tensor(hot_src[:, kk, :, :].rearrange("p n (j c) -> p n j c", j=CPG), iota_src[:, :, :].rearrange("p n (j c) -> p n j c", j=CPG),
                                    turned[:, k, 0, :].rearrange("p (o j g) -> p o j g", o=1, j=CPG)[:, :, :, s * SG:(s + 1) * SG].to_broadcast([P, P, CPG, SG]),
                                    ALU.is_equal).then_inc(hot_ready, 1)

                def key_rows(b, k, s, j):
                    lo, hi = WIN[j]
                    at = j * GROUPS + s * SG
                    one_hot(hot_win[s % 2][j], iota_key[:, lo:hi, :], turned[:, k, 1, at:at + SG]).then_inc(hot_ready, 1)

                def hot_step(b, k, s):
                    source_rows(b, k, s)
                    for j in range(CPG):
                        key_rows(b, k, s, j)

                def rows_of(b, k, turn, ends, following=True, begun=False):
                    if not begun:
                        hot_step(b, k, 0)
                    if following:
                        decode(b + 1, 1 - k, turn * PER + (k + 1) * PER)
                    if not begun:
                        hot_step(b, k, 1)
                    if ends > 1:
                        x1_norm(b - 3, 1 - k, 0)
                    hot_step(b, k, 2)
                    if ends:
                        x1_sum(b - 2, k, 0)
                    hot_step(b, k, 3)
                    if ends:
                        x1_stats(b - 2, k, 0, turn * 16)

                PER = 16 * GROUPS
                between = {LN_TAIL: lambda: decode(0, 0, PER)}
                for s in range(2):
                    at = LN_TAIL + 4 + s * (1 + CPG)
                    between[at] = lambda s=s: source_rows(0, 0, s)
                    for j in range(CPG):
                        between[at + 1 + j] = lambda s=s, j=j: key_rows(0, 0, s, j)
                last_tiles(between)
                rows_of(0, 0, 0, 0, begun=True)
                rows_of(1, 1, 0, 0)
                rows_of(2, 0, 1, 1)
                with dve.Fori(0, (T - 5) // 2) as i:
                    rows_of(i * 2 + 3, 1, i + 1, 2)
                    rows_of(i * 2 + 4, 0, i + 2, 2)
                rows_of(T - 2, 1, (T - 2) // 2, 2)
                rows_of(T - 1, 0, (T - 1) // 2, 2, False)
                x1_norm(T - 3, 0, 0)
                for d in range(T - 2, T):
                    x1_sum(d, d % 2, 0)
                    x1_stats(d, d % 2, 0, (d // 2 + 1) * 16)
                    x1_norm(d, d % 2, 0)
            with dve.Else():
                last_tiles({})
                gs = [0]

                def gstep(ins):
                    gs[0] += 1
                    ins.then_inc(g_pro, 1)

                def gsettled():
                    dve.wait_ge(g_pro, gs[0])

                shape = [P, T, NRANGE]

                def over_blocks(r):
                    return r[:, :].rearrange("p (o g) -> p o g", o=1).to_broadcast(shape)

                node_b = block_node[:, :].rearrange("p (t o) -> p t o", o=1).to_broadcast(shape)
                dve.wait_ge(g_dst_in, 16)
                dve.wait_ge(g_consts, 3)
                gstep(v.tensor_reduce(gmin[:, :], dst_gen[:, :].rearrange("p (g c) -> p g c", c=RANGE), AXX, ALU.min))
                gstep(v.tensor_reduce(gmax[:, :], dst_gen[:, :].rearrange("p (g c) -> p g c", c=RANGE), AXX, ALU.max))
                gsettled()
                gstep(v.tensor_tensor(hit[:, :, :], over_blocks(gmax), node_b, ALU.is_ge))
                gstep(v.tensor_tensor(cand[:, :, :], node_b, over_blocks(gmin), ALU.subtract))
                gsettled()
                gstep(v.scalar_tensor_tensor(out=hit[:, :, :], in0=cand[:, :, :], scalar=float(1 - P), in1=hit[:, :, :], op0=ALU.is_ge, op1=ALU.mult))
                gsettled()
                gstep(v.scalar_tensor_tensor(out=cand[:, :, :], in0=over_blocks(gpos), scalar=-BIG, in1=hit[:, :, :], op0=ALU.add, op1=ALU.mult))
                gsettled()
                gstep(v.tensor_reduce(lim[:, 0, :], cand[:, :, :], AXX, ALU.min))
                gsettled()
                gstep(v.scalar_tensor_tensor(out=cand[:, :, :], in0=over_blocks(gpos), scalar=float(RANGE), in1=hit[:, :, :], op0=ALU.add, op1=ALU.mult))
                gsettled()
                gstep(v.tensor_reduce(lim[:, 1, :], cand[:, :, :], AXX, ALU.max))
                assert gs[0] == G_LIM
                dve.wait_ge(lim_turned, 1)
                gstep(v.tensor_reduce(span[:, 0:1], lim_ps[0][0:T, 0:P], AXX, ALU.min))
                gstep(v.tensor_reduce(span[:, 1:2], lim_ps[1][0:T, 0:P], AXX, ALU.max))
                gsettled()
                gstep(v.scalar_tensor_tensor(out=span[:, 0:1], in0=span[:, 0:1], scalar=BIG, in1=span[:, 1:2], op0=ALU.add, op1=ALU.min))
                gsettled()
                gstep(v.tensor_tensor(span[:, 2:3], span[:, 1:2], span[:, 0:1], ALU.subtract))
                gsettled()
                gstep(v.tensor_scalar(over[:, :], batch_starts[:, :], span[:, 2:3], None, ALU.is_lt, ALU.add, accum_out=span[:, 3:4]))
                gsettled()
                gstep(v.tensor_scalar(span[:, 3:4], span[:, 3:4], 1.0, None, ALU.max))
                assert gs[0] == G_SPAN
                dve.wait_ge(table_made, 1)
                for k in range(3):
                    gstep(v.tensor_copy(table[0:1, k, :], table_ps[k]))
                gsettled()
                dve.sem_inc(table_ready, 1)

                with dve.Fori(0, T) as d:
                    _, n, first = block_edges(dve, d)
                    with dve.Fori(0, n) as j:
                        b = first + j
                        dve.wait_ge(dst_in, (b + 1) * 16)
                        dve.wait_ge(onehot_ready, (b + 1) * U)
                        v.tensor_scalar(dst_loc[:, :], dst_ix[:, :], block_node[:, ds(d, 1)], None, ALU.subtract).then_inc(loc_ready, 1)
                        dve.wait_ge(loc_ready, b + 1)
                        dve.sem_inc(dst_free, 1)
                        for u in range(U):
                            dve.wait_ge(slot_free, b * U + (u + 1))
                            v.tensor_scalar(onehot[:, u, :], iota[:, :], dst_loc[:, u:u + 1], None, ALU.is_equal).then_inc(onehot_ready, 1)
                    x1_sum(d, 0, 1)
                    x1_stats(d, 0, 1, d * 16 + 16)
                    x1_norm(d, 0, 1)

            dve.wait_ge(epi, (T + 2) * EPI)
            v.scalar_tensor_tensor(out=shift[:, :], in0=mean[:, :], scalar=-1.0, in1=rstd[:, :], op0=ALU.mult, op1=ALU.mult).then_inc(shift_ready, 1)

            rs = [0]

            def rstep(ins):
                rs[0] += 1
                ins.then_inc(rt, 1)

            def rsettled():
                dve.wait_ge(rt, rs[0])

            def row(i, n=NX):
                return route[0:1, i, 0:n]

            def softmax(out_row, in_row, n, acts):
                rstep(v.tensor_reduce(row(8, 1), in_row, AXX, ALU.max))
                rsettled()
                rstep(v.tensor_scalar(row(9, n), in_row, row(8, 1), None, ALU.subtract))
                dve.wait_ge(rt_act, acts)
                rstep(v.tensor_reduce(row(8, 1), row(10, n), AXX, ALU.add))
                rsettled()
                rstep(v.reciprocal(row(8, 1), row(8, 1)))
                rsettled()
                rstep(v.tensor_scalar(out_row, row(10, n), row(8, 1), None, ALU.mult))
                rsettled()

            dve.wait_ge(zsum_ready, 1)
            rstep(v.tensor_scalar(zmean[:, :], zsum[:, 0:KD], 1.0 / N, None, ALU.mult))
            dve.wait_ge(rt_pe, 1)
            rstep(v.tensor_tensor(row(0), rt_ps[0:1, 0:NX], br[:, :], ALU.add))
            rsettled()
            softmax(row(1), row(0), NX, 1)
            rstep(v.tensor_scalar(row(2), row(1), float(N), None, ALU.mult))
            rsettled()
            rstep(v.reciprocal(row(3), row(2)))
            rsettled()
            rstep(v.tensor_scalar(row(4), row(3), CAP, 1.0, ALU.mult, ALU.min))
            rsettled()
            rstep(v.tensor_tensor(row(5), row(1), row(4), ALU.mult))
            rsettled()
            softmax(row(6), row(5), NX, 2)
            rstep(v.max(row(7), row(6)))
            rsettled()
            rstep(v.max_index(route_ix[:, :], row(7), row(6)))
            assert rs[0] == ROUTE_IX
            softmax(row(11, TOP_K), row(7, TOP_K), TOP_K, 3)
            assert rs[0] == ROUTE_W
            dve.wait_ge(rt_pe, 2)
            rstep(v.tensor_copy(wts[:, :], rt_ps[:, 64:64 + TOP_K]))
            rsettled()
            def split_z(g, k, n):
                for q in range(KD):
                    dve.wait_ge(zh_kept, g * KD + (KD + q + 1))
                    v.tensor_tensor(zTl[:, k, q, 0:n], zt_ps[q][:, 0:n], zTh[:, k, q, 0:n].bitcast(F32), ALU.subtract).then_inc(zl_kept, 1)

            def split_g(g, k, n):
                for c in range(CF):
                    dve.wait_ge(g_made, g * (2 * CF) + (2 * c + 10))
                    v.tensor_tensor(gl[:, k, c, 0:n], gf[:, c % 2, 0:n], gh[:, k, c, 0:n].bitcast(F32), ALU.subtract).then_inc(gl_made, 1)

            def out_stats(g, k, m):
                t = g * GT + m
                e = t * NORM + 2 * NORM
                dve.wait_ge(y_made, t + (2 * GT + 1))
                dve.wait_ge(prep, g * PREP + (2 * PREP + 1))
                dve.wait_ge(done, t * 2 + (2 * GT + 2))
                v.tensor_tensor(pre[:, m, :], y_ps[(k * GT + m) % 2][:, 0:D], zb[:, k, m, :], ALU.add).then_inc(norm, 1)
                hold(dve, norm, e + 1)
                v.bn_stats(stf[:, m, :], pre[:, m, :]).then_inc(norm, 1)
                hold(dve, norm, e + 2)
                v.bn_aggr(mvf[:, m, :], stf[:, m, :]).then_inc(norm, 1)
                dve.wait_ge(norm, e + 3)
                v.tensor_scalar(vare[:, ds(t, 1)], mvf[:, m, 1:2], LN_EPS, None, ALU.add).then_inc(norm, 1)

            def out_end(g, k, m):
                t = g * GT + m
                v.scalar_tensor_tensor(out=pre[:, m, :], in0=pre[:, m, :], scalar=mvf[:, m, 0:1], in1=gamma_bc[:, :],
                                       op0=ALU.subtract, op1=ALU.mult).then_inc(done, 1)
                dve.wait_ge(pow_ready, t + 1)
                dve.wait_ge(done, t * 2 + (4 * GT + 1))
                dve.wait_ge(prep, g * PREP + (2 * PREP + 2))
                dve.wait_ge(res_free, t + 1)
                v.scalar_tensor_tensor(out=res[:, (k * GT + m) % 2, :], in0=pre[:, m, :], scalar=rstdf[:, ds(t, 1)], in1=x1b[:, k, m, :],
                                       op0=ALU.mult, op1=ALU.add).then_inc(done, 1)

            def output(g, k, n):
                out_stats(g, k, 0)
                for m in range(1, n):
                    out_stats(g, k, m)
                    out_end(g, k, m - 1)
                out_end(g, k, n - 1)

            split_z(0, 0, GT * P)
            for k in range(TOP_K):
                dve.wait_ge(w_split, k + 1)
                rstep(v.tensor_tensor(W1l[:, k, :, :], W1e[:, k, :, :], W1h[:, k, :, :].bitcast(F32), ALU.subtract))
            assert rs[0] == ROUTE_W1 and TOP_K == 2
            split_z(1, 1, GT * P)
            split_g(0, 0, GT * P)
            dve.wait_ge(w_split, 3 * TOP_K)
            rstep(v.tensor_tensor(W2l[:, :, :, :], W2e[:, :, :, :], W2h[:, :, :, :].bitcast(F32), ALU.subtract))
            rstep(v.tensor_scalar(b2w[:, :], b2e[:, 0, :], wts[:, 0:1], None, ALU.mult))
            rsettled()
            rstep(v.scalar_tensor_tensor(out=b2w[:, :], in0=b2e[:, 1, :], scalar=wts[:, 1:2], in1=b2w[:, :],
                                         op0=ALU.mult, op1=ALU.add))
            assert rs[0] == ROUTE_END
            with dve.Fori(0, NG // 2 - 1) as i:
                for k in range(2):
                    split_g(i * 2 + (k + 1), 1 - k, GT * P)
                    split_z(i * 2 + (k + 2), k, GT * P)
                    output(i * 2 + k, k, GT)
            split_g(NG - 1, 1, GT * P)
            split_z(NG, 0, P)
            output(NG - 2, 0, GT)
            split_g(NG, 0, P)
            output(NG - 1, 1, GT)
            output(NG, 0, 1)

        @block.scalar
        def _(act):
            s = nc.scalar
            act.sem_inc(bank_kept, SG)
            act.sem_inc(low_kept, 2)
            act.sem_inc(zh_kept, KD)
            act.sem_inc(g_made, 8)
            xs_done = [0]

            def xstep(ins):
                xs_done[0] += 1
                ins.then_inc(xstat, 1)

            def xsettled():
                act.wait_ge(xstat, xs_done[0])

            act.wait_ge(dve_pro, FALLS)
            s.activation(unused_falls[:, :], falls[:, :], ACT.Copy, accum_out=unsorted[:, :]).then_inc(unsorted_ready, 1)
            for i, (lo, hi) in enumerate(x_parts[:-1]):
                act.wait_ge(x_in[i], 16)
                for t in range(lo, hi):
                    xstep(s.activation(unused[:, t, :], xs[:, t, :], ACT.Copy, accum_out=xsum[:, t:t + 1]))
                xsettled()
                xstep(s.activation(neg_mean[:, lo:hi], xsum[:, lo:hi], ACT.Copy, scale=-1.0 / D))
                xsettled()
                for t in range(lo, hi):
                    xstep(s.activation(unused[:, t, :], xs[:, t, :], ACT.Square, bias=neg_mean[:, t:t + 1], accum_out=xsq[:, t:t + 1]))
            xsettled()
            act.wait_ge(consts, N_CONSTS)
            act.wait_ge(dve_pro, DEG)
            s.activation(sd[:, :], deg_sb[:, :], ACT.Sqrt, bias=ones[:, 0:1]).then_inc(sd_made, 1)
            act.wait_ge(dve_pro, XSTAT)
            s.activation(sd1[:, :], xsq[:, :], ACT.Sqrt, scale=1.0 / D, bias=eps[:, :]).then_inc(sd_made, 1)
            act.wait_ge(dve_pro, DINV)

            def keep_xnT(t, k):
                act.wait_ge(xn_turned, t + 5)
                s.copy(xnT[:, k, :], turn_ps[k][:, 0:D]).then_inc(xnT_ready, 1)

            def keep_h(t, k):
                act.wait_ge(h_made, t + 1)
                s.activation(tile(tab, t)[:, 0:D], h_ps[k][:, 0:D], ACT.Copy, scale=dinv[:, ds(t, 1)]).then_inc(hi_made, 1)

            keep_xnT(0, 0)
            with act.Fori(0, LN_TAIL // 4) as i:
                for m in range(4):
                    keep_xnT(i * 4 + (m + 1), (m + 1) % 2)
                    keep_h(i * 4 + m, m % 2)

            def last_tiles(between=None):
                for t in range(LN_TAIL, T):
                    if t + 1 < T:
                        keep_xnT(t + 1, (t + 1) % 2)
                    keep_h(t, t % 2)
                    if between is not None and t == LN_TAIL + 2:
                        between()
                act.wait_ge(lo_made, T + 2)

            def keep_low(d, k):
                act.wait_ge(acc_ready, d + 1)
                act.wait_ge(low_biased, d + 1)
                s.activation(low[:, :], acc[k][:, D:2 * D], ACT.Copy, scale=dinv[:, ds(d, 1)]).then_inc(low_kept, 1)

            def deviation(d):
                act.wait_ge(epi, d * EPI + (2 * EPI + 6))
                s.copy(mean[:, ds(d, 1)], mvb[:, 0:1]).then_inc(sd2_made, 1)
                s.activation(sd[:, 0:1], mvb[:, 1:2], ACT.Sqrt, bias=eps[:, :]).then_inc(sd2_made, 1)

            with act.If(is_dense(act)):
                def keep_edges(b, k):
                    act.wait_ge(edges_turned, b + 2)
                    s.copy(turned[:, k, :, :].rearrange("p v r -> p (v r)"), edge_ps).then_inc(turned_kept, 1)

                def keep_counts(b, k, s_):
                    for j in range(SG):
                        act.wait_ge(bank_ready, b * (STEPS * SG) + (s_ * SG + j + 1 + 2 * SG))
                        at = (s_ * SG + j) * KEYS
                        s.copy(adj[k][:, at:at + KEYS], adj_ps[j][:, 0:KEYS]).then_inc(bank_kept, 1)

                def counts(b, k, ends, following=True):
                    if ends > 1:
                        deviation(b - 3)
                    if ends:
                        keep_low(b - 2, k)
                    for s_ in range(STEPS):
                        keep_counts(b, k, s_)
                        if s_ == 1 and following:
                            keep_edges(b + 1, 1 - k)

                last_tiles(lambda: keep_edges(0, 0))
                counts(0, 0, 0)
                counts(1, 1, 0)
                counts(2, 0, 1)
                with act.Fori(0, (T - 5) // 2) as i:
                    counts(i * 2 + 3, 1, 2)
                    counts(i * 2 + 4, 0, 2)
                counts(T - 2, 1, 2)
                counts(T - 1, 0, 2, False)
                deviation(T - 3)
                for d in range(T - 2, T):
                    keep_low(d, d % 2)
                    deviation(d)
            with act.Else():
                last_tiles()
                with act.Fori(0, T) as d:
                    keep_low(d, 0)
                    deviation(d)

            for i, (at, n) in enumerate(((4, NX), (13, NX), (20, TOP_K))):
                act.wait_ge(rt, at)
                s.activation(route[0:1, 10, 0:n], route[0:1, 9, 0:n], ACT.Exp).then_inc(rt_act, 1)

            def normalise_again(g, k, n, loaded):
                act.wait_ge(x1_in[k], loaded)
                act.wait_ge(z_turned, g + 1)
                act.wait_ge(prep, g * PREP + PREP)
                for m in range(n):
                    t = g * GT + m
                    s.activation(zf[:, k, m, :], x1f[:, k, m, :], ACT.Identity, scale=rstd[:, ds(t, 1)], bias=shift[:, ds(t, 1)]).then_inc(z_made, 1)

            def keep_z(g, k, n):
                act.wait_ge(z_turned, g + 3)
                for q in range(KD):
                    s.copy(zTh[:, k, q, 0:n], zt_ps[q][:, 0:n]).then_inc(zh_kept, 1)

            def gelus(g, k, n, tiles):
                for c in tiles:
                    if c == 0:
                        act.wait_ge(y_made, g * GT + GT)
                    act.wait_ge(h1_made, g * CF + (c + 1))
                    bias = b1e[:, c // KF, c % KF:c % KF + 1]
                    s.activation(gh[:, k, c, 0:n], h1_ps[c % 4][:, 0:n], ACT.Gelu, bias=bias).then_inc(g_made, 1)
                    act.wait_ge(gl_made, g * CF + (c + 1))
                    s.activation(gf[:, c % 2, 0:n], h1_ps[c % 4][:, 0:n], ACT.Gelu, bias=bias).then_inc(g_made, 1)

            act.wait_ge(shift_ready, 1)
            normalise_again(0, 0, GT, 16)
            normalise_again(1, 1, GT, 16)
            keep_z(0, 0, GT * P)
            act.wait_ge(w1_in, 16 * 2 * TOP_K)
            for k in range(TOP_K):
                s.copy(W1h[:, k, :, :], W1e[:, k, :, :]).then_inc(w_split, 1)
            keep_z(1, 1, GT * P)
            act.wait_ge(rt, ROUTE_WTS)
            act.wait_ge(w2_in, 16 * 2 * TOP_K)
            for k in range(TOP_K):
                s.activation(W2e[:, k, :, :], W2e[:, k, :, :], ACT.Copy, scale=wts[:, k:k + 1]).then_inc(w_split, 1)
            act.wait_ge(w_split, 2 * TOP_K)
            for k in range(TOP_K):
                s.copy(W2h[:, k, :, :], W2e[:, k, :, :]).then_inc(w_split, 1)
            gelus(0, 0, GT * P, range(CF))
            half = CF // 2
            with act.Fori(0, NG // 2 - 1) as i:
                for k in range(2):
                    gelus(i * 2 + (k + 1), 1 - k, GT * P, range(half))
                    normalise_again(i * 2 + (k + 2), k, GT, i * 16 + 32)
                    gelus(i * 2 + (k + 1), 1 - k, GT * P, range(half, CF))
                    keep_z(i * 2 + (k + 2), k, GT * P)
            gelus(NG - 1, 1, GT * P, range(half))
            normalise_again(NG, 0, 1, (NG // 2 + 1) * 16)
            gelus(NG - 1, 1, GT * P, range(half, CF))
            keep_z(NG, 0, P)
            gelus(NG, 0, P, range(CF))

        @block.tensor
        def _(pe):
            mm = nc.tensor.matmul
            pe.sem_inc(xn_turned, 4)
            pe.sem_inc(counted, 2)
            pe.sem_inc(bank_ready, 2 * SG)
            pe.sem_inc(slot_free, U)
            pe.sem_inc(edges_turned, 1)
            pe.sem_inc(z_turned, 2)
            pe.sem_inc(y_made, 2 * GT)
            pe.wait_ge(consts, N_CONSTS + 1)

            pe.wait_ge(unsorted_ready, 1)
            pe.wait_ge(dve_pro, FOUND)
            for i, col in enumerate([unsorted[:, :]] + [overfull[:, i:i + 1] for i in range(SEGS)]):
                last = mm(flag_ps[0:1, 8:9], col, ones[:, 0:1], start=(i == 0), stop=(i == SEGS))
            last.then_inc(runs_checked, 1)

            mm(deg[:, 0:2 * T], zero[:, :], zero[:, 0:2 * T], start=True, stop=True)
            with pe.If(by_runs(pe)):
                def count_runs(c, k):
                    pe.wait_ge(ones_ready, c * 3 + 3)
                    rows_ = hot_run[k].rearrange("p v n c -> p (v n) c")
                    for q in range(SC):
                        last = mm(deg[:, 0:2 * T], hot_src[:, k, :, q], rows_[:, 0:2 * T, q], start=False, stop=True, skip_group_check=True)
                    last.then_inc(counted, 1)

                with pe.Fori(0, RSTEPS // 2) as i:
                    count_runs(i * 2, 0)
                    count_runs(i * 2 + 1, 1)
                pe.wait_ge(counted, RSTEPS + 2)
            with pe.Else():
                def count(c, k):
                    pe.wait_ge(ones_ready, c * 2 + 2)
                    for q in range(SC):
                        last = mm(deg[:, 0:T], hot_src[:, k, :, q], hot_blk[k][:, :, q], start=False, stop=True, skip_group_check=True)
                    last.then_inc(counted, 1)

                with pe.Fori(0, HSTEPS // 2) as i:
                    count(i * 2, 0)
                    count(i * 2 + 1, 1)
                pe.wait_ge(counted, HSTEPS + 2)
            pe.sem_inc(deg_ready, 1)

            def turn_x(t, m):
                pe.wait_ge(xn_ready, t + 1)
                for q in range(KD):
                    last = nc.tensor.transpose(turn_ps[m % 2][:, q * P:(q + 1) * P], xn[m][:, q * P:(q + 1) * P], ident[:, :])
                last.then_inc(xn_turned, 1)

            def make_h(t, k):
                pe.wait_ge(xnT_ready, t + 1)
                pe.wait_ge(lo_made, t + 1)
                for q in range(KD):
                    last = mm(h_ps[k][:, 0:D], xnT[:, k, q * P:(q + 1) * P], W[:, q, :], start=(q == 0), stop=(q == KD - 1))
                last.then_inc(h_made, 1)

            pe.wait_ge(weights_in, N_WEIGHTS)
            turn_x(0, 0)
            pe.wait_ge(dve_pro, DEG)
            mm(cum_ps[0:T, 0:4 * GROUPS + 1], deg_sb[:, :], below[:, :], start=True, stop=True).then_inc(cum_made, 1)
            pe.wait_ge(dve_pro, CUM)
            mm(flag_ps[0:1, 0:1], unsorted[:, :], ones[:, 0:1], start=True, stop=False)
            for i in range(4):
                mm(flag_ps[0:1, 0:1], lost[:, i:i + 1], ones[0:T, 0:1], start=False, stop=(i == 3))
            mm(off_ps[0:T, 0:GROUPS], before[:, :], total[:, :], start=True, stop=True).then_inc(off_made, 1)

            with pe.Fori(0, LN_TAIL // 4) as i:
                for m in range(4):
                    turn_x(i * 4 + (m + 1), (m + 1) % 4)
                    make_h(i * 4 + m, m % 2)

            def last_tiles(between=None):
                for t in range(LN_TAIL, T):
                    if t + 1 < T:
                        turn_x(t + 1, (t + 1) % 4)
                    make_h(t, t % 2)
                    if between is not None and t == LN_TAIL + 2:
                        between()

            pe.wait_ge(flag_ready, 1)
            with pe.If(is_dense(pe)):
                def turn_edges(b, first=False):
                    pe.wait_ge(decoded, b * 4 + 5)
                    if not first:
                        pe.wait_ge(turned_kept, b)
                    for i, row in enumerate((place_row, key_row)):
                        last = mm(edge_ps[:, i * ROWS:(i + 1) * ROWS], row[:, :], order[:, :], start=True, stop=True)
                    last.then_inc(edges_turned, 1)

                def count_edges(b, s):
                    kk = s % 2
                    pe.wait_ge(hot_ready, b * ((1 + CPG) * STEPS) + (1 + CPG) * (s + 1))
                    for g in range(SG):
                        pe.wait_ge(bank_kept, b * (STEPS * SG) + (s * SG + g + 1))
                        for j, (lo, hi) in enumerate(WIN):
                            last = mm(adj_ps[g][:, lo:hi], hot_src[:, kk, :, j * SG + g], hot_win[kk][j][:, :, g],
                                      start=(j == 0), stop=True, skip_group_check=True)
                        last.then_inc(bank_ready, 1)

                def add_rows(k, lo, hi):
                    nodes = adj[k][:, :].rearrange("p (n q) -> p n q", q=T)
                    for q in range(lo, hi):
                        last = mm(acc[k][:, :], nodes[:, :, q], tab[:, q, :], start=(q == 0), stop=(q == T - 1), skip_group_check=True)
                    if hi == T:
                        last.then_inc(acc_ready, 1)

                cuts = [T * s // STEPS for s in range(STEPS + 1)]

                def window(d, k, following, after):
                    for s in range(STEPS):
                        if following:
                            count_edges(d + 1, s)
                        if s == 1 and after:
                            turn_edges(d + 2)
                        if s == 0:
                            pe.wait_ge(loop_added, d + 1)
                            pe.wait_ge(low_kept, d + 1)
                            pe.wait_ge(epi, d * EPI + 1)
                        add_rows(k, cuts[s], cuts[s + 1])

                last_tiles(lambda: turn_edges(0, first=True))
                pe.wait_ge(lo_made, T + 2)
                for s in range(STEPS):
                    count_edges(0, s)
                    if s == 1:
                        turn_edges(1)
                with pe.Fori(0, T // 2 - 1) as i:
                    for k in range(2):
                        window(i * 2 + k, k, True, True)
                window(T - 3, 0, True, True)
                window(T - 2, 1, True, False)
                window(T - 1, 0, False, False)
            with pe.Else():
                last_tiles()
                pe.wait_ge(lo_made, T + 2)
                pe.wait_ge(g_pro, G_LIM)
                for k in range(2):
                    last = nc.tensor.transpose(lim_ps[k][0:T, 0:P], lim[:, k, :], ident[:, :])
                last.then_inc(lim_turned, 1)
                pe.wait_ge(g_pro, G_SPAN)
                for k, (col, mat) in enumerate(((0, ident), (3, ident), (3, before))):
                    last = mm(table_ps[k], span[:, col:col + 1], mat[0:T, 0:T], start=True, stop=True)
                last.then_inc(table_made, 1)

                pe.wait_ge(table_ready, 1)
                with pe.Fori(0, T) as d:
                    _, n, first = block_edges(pe, d)
                    pe.wait_ge(low_kept, d + 2)
                    pe.wait_ge(epi, d * EPI + EPI + 1)
                    mm(acc[0][:, :], ident_r[:, :], tile(tab, d), start=True, stop=True)
                    with pe.Fori(0, n) as j:
                        b = first + j
                        for u in range(U):
                            pe.wait_ge(onehot_ready, b * U + (u + 1 + U))
                            pe.wait_ge(rows_in[u], (b + 1) * 16)
                            mm(acc[0][:, :], onehot[:, u, :], rows[:, u, :], start=False, stop=True, skip_group_check=True).then_inc(slot_free, 1)
                    pe.wait_ge(slot_free, (first + n + 1) * U)
                    pe.sem_inc(acc_ready, 1)

            pe.wait_ge(zsum_done, T + 2)
            for q in range(KD):
                last = mm(zsum[:, q:q + 1], zacc[:, q * P:(q + 1) * P], ones[:, 0:1], start=True, stop=True)
            last.then_inc(zsum_ready, 1)

            pe.wait_ge(rt, 1)
            for q in range(KD):
                last = mm(rt_ps[0:1, 0:NX], zmean[:, q:q + 1], Wr[:, q, :], start=(q == 0), stop=(q == KD - 1))
            last.then_inc(rt_pe, 1)

            def turn_z(g, k, n):
                pe.wait_ge(z_made, g * GT + n)
                pe.wait_ge(zh_kept, g * KD + KD)
                pe.wait_ge(zl_kept, g * KD + KD)
                for m in range(n):
                    for q in range(KD):
                        last = nc.tensor.transpose(zt_ps[q][:, m * P:(m + 1) * P], zf[:, k, m, q * P:(q + 1) * P], ident[:, :])
                last.then_inc(z_turned, 1)

            def hidden(g, k, n):
                pe.wait_ge(zl_kept, g * KD + 2 * KD)
                for e in range(TOP_K):
                    pe.wait_ge(rt, ROUTE_WTS + 1 + e)
                    for f in range(KF):
                        c = e * KF + f
                        pe.wait_ge(g_made, g * (2 * CF) + (2 * c + 2))
                        terms = [(w, z, q) for q in range(KD) for w, z in ((W1h, zTh), (W1h, zTl), (W1l, zTh))]
                        for i, (w, z, q) in enumerate(terms):
                            last = mm(h1_ps[c % 4][:, 0:n], w[:, e, q, f * P:(f + 1) * P], z[:, k, q, 0:n],
                                      start=(i == 0), stop=(i == len(terms) - 1))
                        last.then_inc(h1_made, 1)

            def output(g, k, n):
                pe.wait_ge(rt, ROUTE_END)
                pe.wait_ge(gl_made, g * CF + (CF + 2))
                for m in range(n):
                    pe.wait_ge(norm, (g * GT + m) * NORM + 1)
                    terms = [(x_, w, c) for c in range(CF) for x_, w in ((gh, W2h), (gh, W2l), (gl, W2h))]
                    for i, (x_, w, c) in enumerate(terms):
                        last = mm(y_ps[(k * GT + m) % 2][:, 0:D], x_[:, k, c, m * P:(m + 1) * P], w[:, c // KF, c % KF, :],
                                  start=(i == 0), stop=(i == len(terms) - 1))
                    last.then_inc(y_made, 1)

            turn_z(0, 0, GT)
            pe.wait_ge(rt, ROUTE_W)
            mm(rt_ps[:, 64:64 + TOP_K], ones[0:1, :], route[0:1, 11, 0:TOP_K], start=True, stop=True).then_inc(rt_pe, 1)
            turn_z(1, 1, GT)
            hidden(0, 0, GT * P)
            with pe.Fori(0, NG // 2 - 1) as i:
                for k in range(2):
                    hidden(i * 2 + (k + 1), 1 - k, GT * P)
                    turn_z(i * 2 + (k + 2), k, GT)
                    output(i * 2 + k, k, GT)
            hidden(NG - 1, 1, GT * P)
            turn_z(NG, 0, 1)
            output(NG - 2, 0, GT)
            hidden(NG, 0, P)
            output(NG - 1, 1, GT)
            output(NG, 0, 1)


INPUTS = {"x": "x", "src": "src", "dst": "dst", "L0_gnn_W": "W", "L0_gnn_b": "b", "L0_gnn_prelu_a": "prelu_a",
          "L0_ffn_Wr": "Wr", "L0_ffn_br": "br", "L0_ffn_W1": "W1", "L0_ffn_b1": "b1", "L0_ffn_W2": "W2",
          "L0_ffn_b2": "b2", "L0_ffn_gamma": "gamma", "L0_ffn_beta": "beta"}


def kernel(**inputs):
    import numpy as np
    import concourse.bacc as bacc
    from concourse.bass_utils import run_bass_kernel_spmd

    nc = bacc.Bacc("TRN2", target_bir_lowering=False, num_devices=1)
    n_edges = inputs["src"].shape[0]
    n_nodes = inputs["x"].shape[0]
    n_blocks = -(-n_nodes // P)
    laid_out = {}
    for name, short in INPUTS.items():
        v = np.ascontiguousarray(inputs[name])
        if short in ("src", "dst"):
            nowhere = 0 if short == "src" else n_blocks * P
            v = np.pad(v, (0, padded_edges(n_edges) - n_edges), constant_values=nowhere)
        if short == "x":
            v = np.pad(v, ((0, n_blocks * P - n_nodes), (0, 0)))
        laid_out[short] = v
    laid_out["pairs"] = np.stack([laid_out["src"], laid_out["dst"]], axis=1)
    arrays, args = {}, {}
    for short, v in laid_out.items():
        arrays[f"in_{short}"] = v
        args[short] = nc.dram_tensor(f"in_{short}", v.shape, mybir.dt.from_np(v.dtype), kind="ExternalInput").ap()
    out = nc.dram_tensor("out_0", inputs["x"].shape, F32, kind="ExternalOutput").ap()
    gnn_ffn_kernel(nc, args, out, n_edges)
    r = run_bass_kernel_spmd(nc, [arrays], core_ids=[0])
    return r.results[0]["out_0"]
```
